# Optimizing a Trainium2 kernel written in Bass

```python
import numpy as np
import jax
import jax.numpy as jnp

def _softmax(x, axis=-1):
    return jax.nn.softmax(x, axis=axis)

def _gelu(x):
    return jax.nn.gelu(x, approximate=True)

def _silu(x):
    return jax.nn.silu(x)

def _sigmoid(x):
    return jax.nn.sigmoid(x)

def _layernorm(x, axis=-1, eps=1e-05):
    m = jnp.mean(x, axis=axis, keepdims=True)
    v = jnp.var(x, axis=axis, keepdims=True)
    return (x - m) / jnp.sqrt(v + eps)

def _scatter_add(tgt, idx, src, axis=0):
    return tgt.at[idx].add(src)

def _segment_sum(src, seg, n):
    return jax.ops.segment_sum(src, seg, n)
kernel_name = 'mk_gnn_ffn_d2_gnn_r16_b8f389'

def setup_inputs(seed: int=0):
    np.random.seed(seed)
    _w = jnp.asarray

    def _rec_inputs():
        import jax
        import jax.numpy as jnp
        _gk = jax.random.key(seed)
        x = -8.776e-05 + 1 * jax.random.normal(jax.random.fold_in(_gk, 1), (3125, 256), jnp.float32)
        src = jax.random.randint(jax.random.fold_in(_gk, 2), (100000,), 0, 3125, jnp.int32)
        dst = jnp.minimum((3125 * jax.random.uniform(jax.random.fold_in(_gk, 3), (100000,)) ** 2.0).astype(jnp.int32), 49999)
        _o = jnp.argsort(dst, stable=True)
        src = src[_o]
        dst = dst[_o]
        edge_weight = jax.random.uniform(jax.random.fold_in(_gk, 13), (100000,), jnp.float32, 0.0, 0.999996)
        return (x, src, dst, edge_weight)
    x, src, dst, edge_weight = _rec_inputs()

    def _L0_gnn_setup():
        import jax, jax.numpy as jnp
        import numpy as np
        N_NODES = 1250
        N_EDGES = 20000
        D = 256
        NUM_LAYERS = 5

        def gru_cell(m, h, w_ih, w_hh, b_ih, b_hh):
            gi = m @ w_ih.T + b_ih
            gh = h @ w_hh.T + b_hh
            i_r, i_z, i_n = jnp.split(gi, 3, axis=1)
            h_r, h_z, h_n = jnp.split(gh, 3, axis=1)
            r = jax.nn.sigmoid(i_r + h_r)
            z = jax.nn.sigmoid(i_z + h_z)
            n = jnp.tanh(i_n + r * h_n)
            return (1.0 - z) * n + z * h
        key = jax.random.key(seed)
        ks = jax.random.split(key, 8)
        x = jax.random.normal(ks[0], (N_NODES, D), dtype=jnp.float32)
        src = jax.random.randint(ks[1], (N_EDGES,), 0, N_NODES)
        dst = jax.random.randint(ks[2], (N_EDGES,), 0, N_NODES)
        edge_index = jnp.stack([src, dst]).astype(jnp.int64)
        edge_attr = jax.random.uniform(ks[3], (N_EDGES,), dtype=jnp.float32)
        s = 1.0 / np.sqrt(D)
        weight = jax.random.uniform(ks[4], (NUM_LAYERS, D, D), minval=-s, maxval=s, dtype=jnp.float32)
        w_ih = jax.random.uniform(ks[5], (3 * D, D), minval=-s, maxval=s, dtype=jnp.float32)
        w_hh = jax.random.uniform(ks[6], (3 * D, D), minval=-s, maxval=s, dtype=jnp.float32)
        b = jax.random.uniform(ks[7], (2, 3 * D), minval=-s, maxval=s, dtype=jnp.float32)
        return {'x': x, 'edge_index': edge_index, 'edge_attr': edge_attr, 'weight': weight, 'w_ih': w_ih, 'w_hh': w_hh, 'b_ih': b[0], 'b_hh': b[1]}
    _L0_gnn_all = _L0_gnn_setup()
    _L0_gnn_in = {k: v for k, v in _L0_gnn_all.items() if k in ('weight', 'w_ih', 'w_hh', 'b_ih', 'b_hh')}
    del _L0_gnn_all

    def _L0_ffn_setup():
        import jax, jax.numpy as jnp
        import numpy as np
        C = 256
        HID = 1024
        E = 8
        TEMP = 1.0
        key = jax.random.key(seed)
        ks = jax.random.split(key, 7)
        x = jax.random.normal(ks[0], (8, 1024, C), dtype=jnp.float32)
        W1 = jax.random.normal(ks[1], (C, HID), dtype=jnp.float32) * 0.02
        b1 = jnp.zeros((HID,), dtype=jnp.float32)
        Wg = jax.random.normal(ks[2], (HID, E), dtype=jnp.float32) * 0.02
        bg = jnp.zeros((E,), dtype=jnp.float32)
        Wd = jax.random.normal(ks[3], (E, HID, C), dtype=jnp.float32) * 0.02
        bd = jnp.zeros((E, C), dtype=jnp.float32)
        return {'x': x, 'W1': W1, 'b1': b1, 'Wg': Wg, 'bg': bg, 'Wd': Wd, 'bd': bd}
    _L0_ffn_all = _L0_ffn_setup()
    _L0_ffn_in = {k: v for k, v in _L0_ffn_all.items() if k in ('W1', 'b1', 'Wg', 'bg', 'Wd', 'bd')}
    del _L0_ffn_all

    def _L1_gnn_setup():
        import jax, jax.numpy as jnp
        import numpy as np
        N_NODES = 3125
        N_EDGES = 50000
        IN_F = 256
        HEADS = 8
        D = 32
        ALPHA_SLOPE = 0.2
        EPS = 1e-16
        key = jax.random.key(seed)
        k1, k2, k3, k4, k5 = jax.random.split(key, 5)
        x = jax.random.normal(k1, (N_NODES, IN_F), dtype=jnp.float32)
        W = jax.random.normal(k2, (HEADS, IN_F, D), dtype=jnp.float32) * 0.05
        a = jax.random.normal(k3, (HEADS, 5 * D), dtype=jnp.float32) * 0.05
        src = jax.random.randint(k4, (N_EDGES,), 0, N_NODES, dtype=jnp.int32)
        dst = jax.random.randint(k5, (N_EDGES,), 0, N_NODES, dtype=jnp.int32)
        return {'x': x, 'W': W, 'a': a, 'src': src, 'dst': dst}
    _L1_gnn_all = _L1_gnn_setup()
    _L1_gnn_in = {k: v for k, v in _L1_gnn_all.items() if k in ('W', 'a')}
    del _L1_gnn_all

    def _L1_ffn_setup():
        import jax, jax.numpy as jnp
        import numpy as np
        B, S, H, F, E, K = (8, 256, 256, 512, 16, 2)
        EPS = 1e-05
        key = jax.random.key(seed)
        ks = jax.random.split(key, 9)
        sc = 0.02
        return {'x': jax.random.normal(ks[0], (B, S, H), dtype=jnp.float32), 'gate_w': jax.random.normal(ks[1], (H, E), dtype=jnp.float32) * sc, 'gate_b': jnp.zeros((E,), dtype=jnp.float32), 'w1': jax.random.normal(ks[2], (E, H, F), dtype=jnp.float32) * sc, 'b1': jnp.zeros((E, F), dtype=jnp.float32), 'w2': jax.random.normal(ks[3], (E, F, H), dtype=jnp.float32) * sc, 'b2': jnp.zeros((E, H), dtype=jnp.float32), 'gamma': jnp.ones((H,), dtype=jnp.float32), 'beta': jnp.zeros((H,), dtype=jnp.float32)}
    _L1_ffn_all = _L1_ffn_setup()
    _L1_ffn_in = {k: v for k, v in _L1_ffn_all.items() if k in ('gate_w', 'gate_b', 'w1', 'b1', 'w2', 'b2', 'gamma', 'beta')}
    del _L1_ffn_all
    return {'x': x, 'src': src, 'dst': dst, 'edge_weight': edge_weight, 'L0_gnn_weight': _L0_gnn_in['weight'], 'L0_gnn_w_ih': _L0_gnn_in['w_ih'], 'L0_gnn_w_hh': _L0_gnn_in['w_hh'], 'L0_gnn_b_ih': _L0_gnn_in['b_ih'], 'L0_gnn_b_hh': _L0_gnn_in['b_hh'], 'L0_ffn_W1': _L0_ffn_in['W1'], 'L0_ffn_b1': _L0_ffn_in['b1'], 'L0_ffn_Wg': _L0_ffn_in['Wg'], 'L0_ffn_bg': _L0_ffn_in['bg'], 'L0_ffn_Wd': _L0_ffn_in['Wd'], 'L0_ffn_bd': _L0_ffn_in['bd'], 'L1_gnn_W': _L1_gnn_in['W'], 'L1_gnn_a': _L1_gnn_in['a'], 'L1_ffn_gate_w': _L1_ffn_in['gate_w'], 'L1_ffn_gate_b': _L1_ffn_in['gate_b'], 'L1_ffn_w1': _L1_ffn_in['w1'], 'L1_ffn_b1': _L1_ffn_in['b1'], 'L1_ffn_w2': _L1_ffn_in['w2'], 'L1_ffn_b2': _L1_ffn_in['b2'], 'L1_ffn_gamma': _L1_ffn_in['gamma'], 'L1_ffn_beta': _L1_ffn_in['beta']}

def reference(x, src, dst, edge_weight, L0_gnn_weight, L0_gnn_w_ih, L0_gnn_w_hh, L0_gnn_b_ih, L0_gnn_b_hh, L0_ffn_W1, L0_ffn_b1, L0_ffn_Wg, L0_ffn_bg, L0_ffn_Wd, L0_ffn_bd, L1_gnn_W, L1_gnn_a, L1_ffn_gate_w, L1_ffn_gate_b, L1_ffn_w1, L1_ffn_b1, L1_ffn_w2, L1_ffn_b2, L1_ffn_gamma, L1_ffn_beta):
    import jax
    import jax.numpy as jnp

    def _L0_gnn_ref(x, edge_index, edge_attr, weight, w_ih, w_hh, b_ih, b_hh):
        import jax, jax.numpy as jnp
        import numpy as np
        N_NODES = 1250
        N_EDGES = 20000
        D = 256
        NUM_LAYERS = 5

        def gru_cell(m, h, w_ih, w_hh, b_ih, b_hh):
            gi = m @ w_ih.T + b_ih
            gh = h @ w_hh.T + b_hh
            i_r, i_z, i_n = jnp.split(gi, 3, axis=1)
            h_r, h_z, h_n = jnp.split(gh, 3, axis=1)
            r = jax.nn.sigmoid(i_r + h_r)
            z = jax.nn.sigmoid(i_z + h_z)
            n = jnp.tanh(i_n + r * h_n)
            return (1.0 - z) * n + z * h
        src = edge_index[0]
        dst = edge_index[1]
        n_nodes = x.shape[0]
        h = x
        for i in range(weight.shape[0]):
            m = h @ weight[i]
            msgs = m[src] * edge_attr[:, None]
            agg = jax.ops.segment_sum(msgs, dst, num_segments=n_nodes)
            h = gru_cell(agg, h, w_ih, w_hh, b_ih, b_hh)
        return h

    def _L0_ffn_ref(x, W1, b1, Wg, bg, Wd, bd):
        import jax, jax.numpy as jnp
        import numpy as np
        C = 256
        HID = 1024
        E = 8
        TEMP = 1.0
        orig_shape = x.shape
        xf = x.reshape(-1, orig_shape[-1])
        H = jax.nn.gelu(xf @ W1 + b1, approximate=False)
        probs = jax.nn.softmax((H @ Wg + bg) / TEMP, axis=-1)
        assign = jnp.argmax(probs, axis=-1)
        out = jnp.zeros_like(xf)
        for e in range(Wd.shape[0]):
            y = H @ Wd[e] + bd[e]
            sel = (assign == e)[:, None]
            out = out + jnp.where(sel, probs[:, e:e + 1] * y, 0.0)
        return out.reshape(orig_shape)

    def _L1_gnn_ref(x, W, a, src, dst):
        import jax, jax.numpy as jnp
        import numpy as np
        N_NODES = 3125
        N_EDGES = 50000
        IN_F = 256
        HEADS = 8
        D = 32
        ALPHA_SLOPE = 0.2
        EPS = 1e-16
        n = x.shape[0]
        h = jnp.einsum('ni,hio->nho', x, W)
        hs = h[src]
        hd = h[dst]
        diff = hd - hs
        a1, a2, a3, a4, a5 = jnp.split(a, 5, axis=1)
        lin = jnp.einsum('ehd,hd->eh', hs, a1) + jnp.einsum('ehd,hd->eh', hd, a2) + jnp.einsum('ehd,hd->eh', diff, a3) + jnp.einsum('ehd,hd->eh', jnp.abs(diff), a4) + jnp.einsum('ehd,hd->eh', hs * hd, a5)
        alpha = jnp.where(lin > 0, lin, ALPHA_SLOPE * lin)
        mx = jax.ops.segment_max(alpha, src, num_segments=n)
        e = jnp.exp(alpha - mx[src])
        s = jax.ops.segment_sum(e, src, num_segments=n)
        att = e / (s[src] + EPS)
        out = jax.ops.segment_sum(att[..., None] * hd, src, num_segments=n)
        return out.reshape(n, HEADS * D)

    def _L1_ffn_ref(x, gate_w, gate_b, w1, b1, w2, b2, gamma, beta):
        import jax, jax.numpy as jnp
        import numpy as np
        B, S, H, F, E, K = (8, 256, 256, 512, 16, 2)
        EPS = 1e-05
        gate_logits = x @ gate_w + gate_b
        topk_vals, topk_idx = jax.lax.top_k(gate_logits, K)
        topk_w = jax.nn.softmax(topk_vals, axis=-1)
        h = jax.nn.relu(jnp.einsum('bsh,ehf->bsef', x, w1) + b1)
        expert_out = jnp.einsum('bsef,efh->bseh', h, w2) + b2
        sel = jnp.take_along_axis(expert_out, topk_idx[:, :, :, None], axis=2)
        moe = jnp.sum(topk_w[..., None] * sel, axis=2)
        y = x + moe
        mu = jnp.mean(y, axis=-1, keepdims=True)
        var = jnp.var(y, axis=-1, keepdims=True)
        return (y - mu) / jnp.sqrt(var + EPS) * gamma + beta
    edge_index = jnp.stack([src, dst])
    x = x + _L0_gnn_ref(_layernorm(x, axis=-1), edge_index, edge_weight, L0_gnn_weight, L0_gnn_w_ih, L0_gnn_w_hh, L0_gnn_b_ih, L0_gnn_b_hh)
    x = x + _L0_ffn_ref(_layernorm(x, axis=-1)[None], L0_ffn_W1, L0_ffn_b1, L0_ffn_Wg, L0_ffn_bg, L0_ffn_Wd, L0_ffn_bd)[0]
    x = x + _L1_gnn_ref(_layernorm(x, axis=-1), L1_gnn_W, L1_gnn_a, src, dst)
    x = x + _L1_ffn_ref(_layernorm(x, axis=-1)[None], L1_ffn_gate_w, L1_ffn_gate_b, L1_ffn_w1, L1_ffn_b1, L1_ffn_w2, L1_ffn_b2, L1_ffn_gamma, L1_ffn_beta)[0]
    return x

_drawn_inputs = setup_inputs


def setup_inputs(seed=0):
    import zlib

    import numpy as np

    out = dict(_drawn_inputs(seed))
    spreads = {'L0_ffn_b1': (0.0, 0.63),
     'L0_ffn_bg': (0.0, 0.378),
     'L0_ffn_bd': (0.0, 0.561),
     'L1_ffn_gate_b': (0.0, 0.284),
     'L1_ffn_b1': (0.0, 0.763),
     'L1_ffn_b2': (0.0, 0.1),
     'L1_ffn_gamma': (1.0, 0.2),
     'L1_ffn_beta': (0.0, 0.1)}
    factors = {'L0_ffn_W1': 2.827, 'L0_ffn_Wg': 3.098, 'L0_ffn_Wd': 3.414}
    for name, (base, spread) in spreads.items():
        noise = np.random.default_rng([zlib.crc32(name.encode()), seed]).standard_normal(out[name].shape)
        drawn = base * np.exp(spread * noise) if base else spread * noise
        out[name] = jnp.asarray(drawn.astype(out[name].dtype))
    for name, factor in factors.items():
        out[name] = (out[name] * factor).astype(out[name].dtype)
    return out
```

```python
import numpy as np
import concourse.bass as bass
from concourse import mybir
from contextlib import ExitStack

F32 = mybir.dt.float32
I32 = mybir.dt.int32
BF = mybir.dt.bfloat16
ALU = mybir.AluOpType
ACT = mybir.ActivationFunctionType
AX = mybir.AxisListType.X

N = 3125
NB = 25
TAIL = N - 24 * 128
D = 256
E = 100000
T1 = 782
T2 = 832
NPAIR = 415
PADKEY = 8000
NG = 7
AROW = NB * 512
ASIZE = NG * 128 * AROW
BIG = 1.0e30


class Sem:
    def __init__(self, handle):
        self.handle = handle
        self.n = 0

    def add(self, ins, k):
        ins.then_inc(self.handle, k)
        self.n += k
        return self, self.n


class Eng:

    def __init__(self, e, new_sem):
        self.e = e
        self.new_sem = new_sem
        self.sem = new_sem()
        self.seen = {}

    def w(self, *ticks):
        for s, v in ticks:
            if self.seen.get(s, 0) < v:
                self.e.wait_ge(s.handle, v)
                self.seen[s] = v
        return self.e

    def did(self, ins):
        if self.sem.n >= 20000:
            self.sem = self.new_sem()
        return self.sem.add(ins, 1)

    def last(self):
        return [(self.sem, self.sem.n)] if self.sem.n else []


def program(nc, a, out, stop=99, dbg=None):
    ctx = ExitStack()
    with ctx:
        names = [0]

        def new_sem():
            names[0] += 1
            return Sem(ctx.enter_context(nc.semaphore(f"s{names[0]}")))

        V, A, T, G, S = (Eng(e, new_sem) for e in (nc.vector, nc.scalar, nc.tensor, nc.gpsimd, nc.sync))
        engines = (V, A, T, G, S)
        MEMW = 52800
        mem = ctx.enter_context(nc.sbuf_tensor("mem", [128, MEMW], F32))
        PS = ctx.enter_context(nc.psum_tensor("PS", [128, 8, 512], F32))
        top = [0]

        def mk(*dims, dt=F32):
            n = 1
            for d in dims:
                n *= d
            words = n if dt != BF else (n + 1) // 2
            o = top[0]
            top[0] += words
            assert top[0] <= MEMW, top[0] * 4
            v = mem[:, o:o + words]
            if dt != F32:
                v = v.bitcast(dt)
            if dt == BF and n % 2:
                v = v[:, 0:n]
            if len(dims) == 2:
                v = v.rearrange("p (a b) -> p a b", a=dims[0])
            if len(dims) == 3:
                v = v.rearrange("p (a b c) -> p a b c", a=dims[0], b=dims[1])
            return v

        def dram(name, shape, dt):
            return nc.dram_tensor(name, shape, dt, kind="Internal").ap()

        def load(q, dst, src, sem, *ticks, **kw):
            return sem.add(q.w(*ticks).dma_start(dst, src, **kw), 16)

        def meet(*ticks):
            ends = [t for g in engines for t in g.last()] + list(ticks)
            for g in engines:
                g.w(*ends)

        def bc(ap, shape):
            return ap.broadcast_to(shape)

        def probe(name, ap, *ticks):
            if dbg is not None and name in dbg:
                s = new_sem()
                o = nc.dram_tensor("dbg_" + name, list(ap.shape), ap.dtype, kind="ExternalOutput").ap()
                tk = load(S, o, ap, s, *(list(ticks) + [t for g in engines for t in g.last()]))
                S.w(tk)
                meet(tk)

        SA = dram("sorted_by_dst", (128 * T1, 4), I32)
        SB = dram("sorted_by_src", (128 * T2, 4), I32)
        AD = dram("adjacency", (ASIZE, 1), F32)
        HD = dram("gat_rows", (NB * 128, 272), F32)
        Q1 = dram("carry_in", (128, 4), F32)
        Q2 = dram("carry_fwd", (128, 1), F32)
        Q3 = dram("carry_mid", (128, 1), F32)
        Q4 = dram("carry_bwd", (128, 1), F32)

        cst = mk(5, 128)
        ident, iota, lowt, upt, ones = (cst[:, i, :] for i in range(5))
        pidx = mk(1)
        epsc = mk(1)
        pairs = mk(T2 // 2)
        identb = mk(128, dt=BF)
        iotab = mk(128, dt=BF)
        recB = mk(T2, 4, dt=I32)
        blko = mk(T2 // 2, dt=I32)
        blkf = mk(T2 // 2)
        base_top = top[0]

        s_c = new_sem()
        load(S, cst[:, :, :], a["c_sq"], s_c)
        load(S, pairs, a["c_pairs"], s_c)
        load(S, pidx, a["c_pidx"], s_c)
        tc = load(S, epsc, a["c_eps"], s_c)
        V.did(V.w(tc).tensor_copy(identb, ident))
        tk = V.did(V.e.tensor_copy(iotab, iota))
        for g in engines:
            g.w(tc, tk)

        padt = recB
        zt = mk(1600)
        tz = G.did(G.e.memset(zt, 0.0))
        tp = G.did(G.e.memset(padt[:, :, 2:4], 0))
        tp = G.did(G.w(tp).memset(padt[:, :, 0:2], PADKEY))
        s_pad = new_sem()
        load(S, SA.rearrange("(p t) f -> p (t f)", p=128), padt[:, 0:T1, :].rearrange("p t f -> p (t f)"), s_pad, tp)
        t_pad = load(S, SB.rearrange("(p t) f -> p (t f)", p=128), padt[:, :, :].rearrange("p t f -> p (t f)"), s_pad)
        s_zero = new_sem()
        av = AD.rearrange("(k p n) o -> k p (n o)", p=128, n=1600)
        for k in range(ASIZE // (128 * 1600)):
            t_zero = load(A, av[k], zt, s_zero, tz)

        def sort(P, NC, rec, kc, t_rec, dest, TT, drop, aligned):
            mark = top[0]
            tmpi = mk(NC, dt=I32)
            keyf = mk(NC)
            lob, hib, h128 = (mk(NC, dt=BF) for _ in range(3))
            Ohi = mk(NC, 25, dt=BF)
            H = mk(25, NC + 1)
            Olo = [mk(20, 128, dt=BF) for _ in range(2)]
            tot = mk(25)
            toti = mk(25, dt=I32)
            inc = mk(25)
            off = mk(25)
            key = rec[:P, :, kc]
            V.did(V.w(t_rec).tensor_copy(keyf[:P], key))
            tk = V.did(V.e.tensor_single_scalar(tmpi[:P], key, 127, ALU.bitwise_and))
            tk = V.did(V.w(tk).tensor_copy(lob[:P], tmpi[:P]))
            tk = V.did(V.w(tk).tensor_single_scalar(tmpi[:P], key, 7, ALU.logical_shift_right))
            tk = V.did(V.w(tk).tensor_copy(hib[:P], tmpi[:P]))
            tk = V.did(V.w(tk).tensor_scalar(h128[:P], tmpi[:P], 128.0, None, ALU.mult))
            tk = V.did(V.w(tk).tensor_tensor(Ohi[:P], bc(hib[:P].unsqueeze(2), [P, NC, 25]),
                                             bc(iotab[:P, 0:25].unsqueeze(1), [P, NC, 25]), ALU.is_equal))
            t_ohi = tk
            groups = [(c, min(20, NC - c)) for c in range(0, NC, 20)]
            t_mm, t_ev = {}, {}
            for g, (c0, n) in enumerate(groups):
                ol = Olo[g % 2][:P, 0:n, :]
                w = [t_mm[g - 2]] if g >= 2 else []
                t_ol = V.did(V.w(t_ohi, *w).tensor_tensor(
                    ol, bc(lob[:P, c0:c0 + n].unsqueeze(2), [P, n, 128]),
                    bc(iotab[:P].unsqueeze(1), [P, n, 128]), ALU.is_equal))
                T.w(t_ol, *([t_ev[g - 2]] if g >= 2 else []))
                for j in range(n):
                    ins = T.e.matmul(PS[:, g % 2, j * 25:(j + 1) * 25], lhsT=ol[:, j, :],
                                     rhs=Ohi[:P, c0 + j, :], start=True, stop=True)
                t_mm[g] = T.did(ins)
                t_ev[g] = A.did(A.w(t_mm[g]).activation(
                    H[:, :, 1 + c0:1 + c0 + n],
                    PS[:, g % 2, 0:n * 25].rearrange("p (j b) -> p b j", b=25), ACT.Copy))
            tk = V.did(V.w(t_ev[len(groups) - 1], t_ev[len(groups) - 2]).tensor_reduce(
                tot, H[:, :, 1:NC + 1], AX, ALU.add))
            T.w(tk).matmul(PS[:, 2, 0:25], lhsT=upt, rhs=tot, start=True, stop=True)
            t_tot = T.did(T.e.matmul(PS[:, 3, 0:25], lhsT=ones, rhs=tot, start=True, stop=True))
            if aligned:
                tk = V.did(V.w(t_tot).tensor_scalar(tot, PS[:, 3, 0:25], 255.0, None, ALU.add))
                tk = V.did(V.w(tk).tensor_copy(toti, tot))
                tk = V.did(V.w(tk).tensor_single_scalar(toti, toti, 8, ALU.logical_shift_right))
                tk = V.did(V.w(tk).tensor_copy(tot, toti))
                tk = V.did(V.w(tk).tensor_scalar(tot, tot, 256.0, None, ALU.mult))
            else:
                tk = V.did(V.w(t_tot).tensor_copy(tot, PS[:, 3, 0:25]))
            tk = V.did(V.w(tk).tensor_tensor_scan(inc, ones[:, 0:25], tot, 0.0, ALU.mult, ALU.add))
            tk = V.did(V.w(tk).tensor_tensor(inc, inc, tot, ALU.subtract))
            tk = t_inc = V.did(V.w(tk).tensor_tensor(off, inc, PS[:, 2, 0:25], ALU.add))
            for b in range(25):
                V.did(V.w(tk).tensor_copy(H[:, b, 0:1], off[:, b:b + 1]))
                t_scan = V.did(V.e.tensor_tensor_scan(H[:, b, 1:NC + 1], bc(ones[:, 0:1], [128, NC]), H[:, b, 1:NC + 1],
                                                      off[:, b:b + 1], ALU.mult, ALU.add))
            if aligned:
                tk = V.did(V.w(t_inc).tensor_scalar(inc, inc, 1.0 / 256.0, None, ALU.mult))
                tk = V.did(V.w(tk).tensor_scalar(blkf, pairs, inc[:, 1:2], None, ALU.is_ge))
                for b in range(2, 25):
                    tk = V.did(V.w(tk).scalar_tensor_tensor(blkf, pairs, inc[:, b:b + 1], blkf, ALU.is_ge, ALU.add))
            top_h = top[0]
            OT = [mk(4, 128) for _ in range(2)]
            R = mk(NC)
            B = mk(NC)
            junk = [mk(128) for _ in range(4)]
            t_jk = {}
            tmp = mk(20, 25)
            posi = mk(NC, dt=I32)
            rowi = mk(NC, dt=I32)
            padf = mk(NC)
            if drop:
                tk = V.did(V.w(t_rec).tensor_scalar(padf[:P], keyf[:P], 4000.0, 1.0e6, ALU.is_ge, ALU.mult))
                t_padf = tk
            nsub = (NC + 3) // 4
            t_lr, t_kr, t_ot, t_rk, t_bs, t_cmb = {}, {}, {}, {}, {}, {}
            s_scat = new_sem()
            t_idx_done = None

            def cols(s):
                return range(4 * s, min(4 * s + 4, NC))

            def base(s):
                T.w(t_ot[s], t_scan)
                for c in cols(s):
                    g, j = c // 20, c % 20
                    if j == 0 and g >= 2:
                        T.w(t_cmb[g - 2])
                    ins = T.e.matmul(PS[:P, 4 + g % 2, j * 25:(j + 1) * 25], lhsT=OT[s % 2][:, c % 4, 0:P],
                                     rhs=H[:, :, c], start=True, stop=True)
                t_bs[s] = T.did(ins)

            def finish(c0, c1):
                w = slice(c0, c1)
                tk = V.did(V.w(t_rk[(c1 - 1) // 4], t_cmb[(c1 - 1) // 20]).tensor_tensor(
                    B[:P, w], B[:P, w], R[:P, w], ALU.add))
                tk = V.did(V.w(tk).tensor_copy(posi[:P, w], B[:P, w]))
                V.did(V.w(tk).tensor_single_scalar(rowi[:P, w], posi[:P, w], 127, ALU.bitwise_and))
                tk = V.did(V.e.tensor_single_scalar(posi[:P, w], posi[:P, w], 7, ALU.logical_shift_right))
                tk = V.did(V.w(tk).tensor_copy(B[:P, w], rowi[:P, w]))
                tk = V.did(V.w(tk).tensor_copy(R[:P, w], posi[:P, w]))
                tk = V.did(V.w(tk).scalar_tensor_tensor(B[:P, w], B[:P, w], float(TT), R[:P, w], ALU.mult, ALU.add))
                if drop:
                    tk = V.did(V.w(tk).tensor_tensor(B[:P, w], B[:P, w], padf[:P, w], ALU.add))
                tk = V.did(V.w(tk).tensor_copy(rowi[:P, w], B[:P, w]))
                G.w(tk, t_pad)
                for c in range(c0, c1):
                    r = s_scat.add(G.e.indirect_dma_start(
                        dest[:, :], bass.IndirectOffsetOnAxis(ap=rowi[:P, c:c + 1], axis=0), rec[:P, c, :], None,
                        bounds_check=128 * TT - 1, oob_is_err=False), 16)
                return r

            done = 0
            for s in range(nsub + 1):
                if s < nsub:
                    T.w(t_ohi, *([t_ot[s - 2], t_rk[s - 2]] if s >= 2 else [t_tot, t_scan]))
                    for c in cols(s):
                        j = c % 4
                        lo = bc(lob[:P, c:c + 1], [P, 128])
                        hi = bc(h128[:P, c:c + 1], [P, 128])
                        T.e.matmul(PS[:, s % 2, j * 128:j * 128 + P], lhsT=lo, rhs=identb[:P, :P], start=True, stop=True)
                        T.e.matmul(PS[:, 2 + s % 2, j * 128:j * 128 + P], lhsT=hi, rhs=identb[:P, :P], start=True, stop=False)
                        ins = T.e.matmul(PS[:, 2 + s % 2, j * 128:j * 128 + P], lhsT=lo, rhs=identb[:P, :P],
                                         start=False, stop=True)
                    t_lr[s] = T.did(ins)
                    n = len(cols(s))
                    lr = PS[:, s % 2, 0:n * 128].rearrange("p (j e) -> p j e", e=128)[:, :, 0:P]
                    t_ot[s] = V.did(V.w(t_lr[s], *([t_bs[s - 2]] if s >= 2 else [])).tensor_scalar(
                        OT[s % 2][:, 0:n, 0:P], lr, pidx, None, ALU.is_equal))
                    for c in cols(s):
                        j = c % 4
                        t_rk[s] = t_jk[c] = V.did(V.w(*([t_jk[c - 4]] if c >= 4 else [])).scalar_tensor_tensor(
                            junk[j][:P, 0:P], PS[:P, 2 + s % 2, j * 128:j * 128 + P], keyf[:P, c:c + 1],
                            lowt[:P, 0:P], ALU.is_equal, ALU.mult, accum_out=R[:P, c:c + 1]))
                if s >= 1:
                    base(s - 1)
                    c1 = min(4 * s, NC)
                    if c1 % 20 == 0 or c1 == NC:
                        g = (c1 - 1) // 20
                        c0, n = groups[g]
                        tk = V.did(V.w(t_bs[s - 1], *([t_cmb[g - 1]] if g else [])).tensor_tensor(
                            tmp[:P, 0:n, :], PS[:P, 4 + g % 2, 0:n * 25].rearrange("p (j b) -> p j b", b=25),
                            Ohi[:P, c0:c0 + n, :], ALU.mult))
                        t_cmb[g] = V.did(V.w(tk).tensor_reduce(B[:P, c0:c0 + n], tmp[:P, 0:n, :], AX, ALU.add))
                        if c1 - done >= 100 or c1 == NC:
                            t_all = finish(done, c1)
                            done = c1
            top[0] = mark
            return t_all

        rec0 = mk(800, 4, dt=I32)
        hi_mem = mem[:, MEMW - 2400:MEMW]
        srt, drt = hi_mem[:, 0:800].bitcast(I32), hi_mem[:, 800:1600].bitcast(I32)
        wrt = hi_mem[:, 1600:2400]
        s_in = new_sem()
        load(S, srt[:125], a["src"].rearrange("(p c) -> p c", p=125), s_in)
        load(S, drt[:125], a["dst"].rearrange("(p c) -> p c", p=125), s_in)
        ti = load(S, wrt[:125], a["edge_weight"].rearrange("(p c) -> p c", p=125), s_in)
        V.did(V.w(ti).memset(rec0[:125, :, 3:4], 0))
        V.did(V.e.tensor_copy(rec0[:125, :, 0], srt[:125]))
        V.did(V.e.tensor_copy(rec0[:125, :, 1], drt[:125]))
        tr = V.did(V.e.tensor_copy(rec0[:125, :, 2].bitcast(F32), wrt[:125]))
        tall = sort(125, 800, rec0[:125], 1, tr, SA, T1, False, False)
        meet(tall, t_zero, t_pad)
        top[0] = base_top
        rec1 = mk(T1, 4, dt=I32)
        s_in2 = new_sem()
        ti = load(S, rec1.rearrange("p t f -> p (t f)"), SA.rearrange("(p t) f -> p (t f)", p=128), s_in2)
        probe("rec1", rec1, ti)
        if stop <= 1:
            S.w(ti, t_zero)
            return
        tall = sort(128, T1, rec1, 0, ti, SB, T2, True, True)
        meet(tall)
        top[0] = base_top
        t_rec = load(S, recB.rearrange("p t f -> p (t f)"), SB.rearrange("(p t) f -> p (t f)", p=128), s_in2)
        probe("recB", recB, t_rec)
        probe("blkf", blkf)
        if stop <= 2:
            S.w(t_rec, t_zero)
            return

        SF = mk(T2)
        NLF = mk(T2)
        aidx = mk(T2, dt=I32)
        keep_top = top[0]
        ia, ib = mk(T2, dt=I32), mk(T2, dt=I32)
        fa, fb, keyf = mk(T2), mk(T2), mk(T2)
        KT = mk(1026)
        WT = mk(1024)
        EQ = mk(1025)
        SX = mk(1024)
        rows = mk(6, 104)
        cinc = mk(1)
        aone = mk(1)
        srcc, dstc, wc = recB[:, :, 0], recB[:, :, 1], recB[:, :, 2].bitcast(F32)
        tk = V.did(V.w(t_rec).tensor_copy(fa, srcc))
        tk2 = V.did(V.e.tensor_copy(fb, dstc))
        tk = V.did(V.w(tk, tk2).scalar_tensor_tensor(keyf, fa, 4096.0, fb, ALU.mult, ALU.add))
        kv = keyf.rearrange("p (a g) -> p g a", g=8)
        wv = recB[:, :, 2].bitcast(F32).rearrange("p (a g) -> p g a", g=8)
        T.w(tk, t_rec)
        for g in range(8):
            T.e.transpose(PS[0:104, g // 4, (g % 4) * 128:(g % 4) * 128 + 128], kv[:, g, :], ident)
            ins = T.e.transpose(PS[0:104, 2 + g // 4, (g % 4) * 128:(g % 4) * 128 + 128], wv[:, g, :], ident)
        tt = T.did(ins)
        ta = A.did(A.w(tt).activation(KT[0:104, 1:1025].rearrange("p (b n) -> p b n", b=2), PS[0:104, 0:2, :], ACT.Copy))
        tb = V.did(V.w(tt).tensor_copy(WT[0:104].rearrange("p (b n) -> p b n", b=2), PS[0:104, 2:4, :]))
        T.w(ta).transpose(PS[0:1, 4, 0:104], KT[0:104, 1:2], ident[0:104, 0:104])
        tt = T.did(T.e.transpose(PS[0:1, 4, 128:232], KT[0:104, 1024:1025], ident[0:104, 0:104]))
        t0 = V.did(V.e.memset(rows[0:1, :, :], -1.0))
        V.did(V.w(tt, t0).tensor_copy(rows[0:1, 0, 1:104], PS[0:1, 4, 128:231]))
        tk = V.did(V.e.tensor_copy(rows[0:1, 1, 0:103], PS[0:1, 4, 1:104]))
        T.w(tk).transpose(PS[0:104, 5, 0:1], rows[0:1, 0, :], ident[0:1, 0:1])
        tt = T.did(T.e.transpose(PS[0:104, 5, 1:2], rows[0:1, 1, :], ident[0:1, 0:1]))
        V.did(V.w(tt, ta).tensor_copy(KT[0:104, 0:1], PS[0:104, 5, 0:1]))
        tk = V.did(V.e.tensor_copy(KT[0:104, 1025:1026], PS[0:104, 5, 1:2]))
        tk = V.did(V.w(tk).tensor_tensor(EQ[0:104], KT[0:104, 1:1026], KT[0:104, 0:1025], ALU.is_equal))
        t1 = V.did(V.w(tk, tb).tensor_tensor_scan(SX[0:104], EQ[0:104, 0:1024], WT[0:104], 0.0, ALU.mult, ALU.add))
        t2 = V.did(V.e.tensor_reduce(aone[0:104], EQ[0:104, 1:1024], AX, ALU.min))
        T.w(t1, t2).transpose(PS[0:1, 6, 0:104], SX[0:104, 1023:1024], ident[0:104, 0:104])
        T.e.transpose(PS[0:1, 6, 128:232], aone[0:104], ident[0:104, 0:104])
        tt = T.did(T.e.transpose(PS[0:1, 6, 256:360], EQ[0:104, 0:1], ident[0:104, 0:104]))
        V.did(V.w(tt).tensor_copy(rows[0:1, 2, :], PS[0:1, 6, 0:104]))
        tk = V.did(V.e.tensor_copy(rows[0:1, 3, :], PS[0:1, 6, 128:232]))
        tk = V.did(V.w(tk).tensor_tensor(rows[0:1, 3, :], rows[0:1, 3, :], PS[0:1, 6, 256:360], ALU.mult))
        tk = V.did(V.w(tk).tensor_tensor_scan(rows[0:1, 4, :], rows[0:1, 3, :], rows[0:1, 2, :], 0.0, ALU.mult, ALU.add))
        tk0 = V.did(V.e.memset(rows[0:1, 5, 0:1], 0.0))
        tk = V.did(V.w(tk, tk0).tensor_copy(rows[0:1, 5, 1:104], rows[0:1, 4, 0:103]))
        tt = T.did(T.w(tk).transpose(PS[0:104, 5, 2:3], rows[0:1, 5, :], ident[0:1, 0:1]))
        tk = V.did(V.w(tt).tensor_copy(cinc[0:104], PS[0:104, 5, 2:3]))
        tk = V.did(V.w(tk).tensor_tensor_scan(SX[0:104], EQ[0:104, 0:1024], WT[0:104], cinc[0:104], ALU.mult, ALU.add))
        T.w(tk)
        for g in range(8):
            T.e.transpose(PS[:, g // 4, (g % 4) * 128:(g % 4) * 128 + 104], SX[0:104, g * 128:(g + 1) * 128], ident[0:104, 0:104])
            ins = T.e.transpose(PS[:, 2 + g // 4, (g % 4) * 128:(g % 4) * 128 + 104],
                                EQ[0:104, 1 + g * 128:1 + (g + 1) * 128], ident[0:104, 0:104])
        tt = T.did(ins)

        def back(bank):
            return PS[:, bank, :].rearrange("p (g a) -> p g a", g=4)[:, :, 0:104]

        sfv = SF.rearrange("p (a g) -> p g a", g=8)
        nlv = NLF.rearrange("p (a g) -> p g a", g=8)
        for h in range(2):
            t_sf = A.did(A.w(tt).activation(sfv[:, 4 * h:4 * h + 4, :], back(h), ACT.Copy))
            t_nl = V.did(V.w(tt).tensor_copy(nlv[:, 4 * h:4 * h + 4, :], back(2 + h)))
        tk = V.did(V.e.tensor_single_scalar(ia, srcc, 127, ALU.bitwise_and))
        t2 = V.did(V.e.tensor_single_scalar(ib, srcc, 7, ALU.logical_shift_right))
        tk = V.did(V.w(tk).tensor_copy(fa, ia))
        t2 = V.did(V.w(t2).tensor_copy(fb, ib))
        tk = V.did(V.w(tk, t2).tensor_scalar(fa, fa, float(AROW), None, ALU.mult))
        tk = V.did(V.w(tk).scalar_tensor_tensor(fa, fb, 512.0, fa, ALU.mult, ALU.add))
        V.did(V.w(tk).tensor_single_scalar(ia, dstc, 511, ALU.bitwise_and))
        t2 = V.did(V.e.tensor_single_scalar(ib, dstc, 9, ALU.logical_shift_right))
        t2 = V.did(V.w(t2).tensor_copy(fb, ib))
        tk = V.did(V.w(t2).scalar_tensor_tensor(fa, fb, float(128 * AROW), fa, ALU.mult, ALU.add))
        t2 = V.did(V.w(tk).tensor_copy(fb, ia))
        tk = V.did(V.w(t2).tensor_tensor(fa, fa, fb, ALU.add))
        tk = V.did(V.w(tk, t_nl).scalar_tensor_tensor(fa, NLF, 16777216.0, fa, ALU.mult, ALU.add))
        tk = V.did(V.w(tk).tensor_copy(aidx, fa))
        G.w(tk, t_zero, t_sf)
        s_adj = new_sem()
        for t in range(2 * NPAIR):
            t_adj = s_adj.add(G.e.indirect_dma_start(
                AD[:, :], bass.IndirectOffsetOnAxis(ap=aidx[:, t:t + 1], axis=0), SF[:, t:t + 1], None,
                bounds_check=ASIZE - 1, oob_is_err=False), 16)
        probe("SF", SF, t_adj)
        probe("aidx", aidx, t_adj)
        if stop <= 3:
            S.w(t_adj)
            return
        meet()
        top[0] = keep_top

        def rows_of(b):
            return TAIL if b == NB - 1 else 128

        def cols_of(q):
            return (TAIL + 3) // 4 * 4 if q == NG - 1 else 512

        def load_rows(dst, src, q, sem, *ticks):
            load(q, dst[:, 0:24, :], src[0:3072, :].rearrange("(b p) d -> p b d", p=128), sem, *ticks)
            return load(q, dst[0:TAIL, 24, :], src[3072:N, :], sem)

        def layernorm(dst, src, t_src):
            st = mk(NB, 6)
            mv = mk(NB, 2)
            sd = mk(NB)
            ticks = {}
            for b in range(NB):
                ticks[b] = V.did(V.w(*t_src).bn_stats(st[:, b, :], src[:, b, :]))
            for b in range(NB):
                tk = V.did(V.w(ticks[b]).bn_aggr(mv[:, b, :], st[:, b, :]))
            tk = A.did(A.w(tk).activation(sd, mv[:, :, 1], ACT.Sqrt, bias=epsc))
            tk = V.did(V.w(tk).reciprocal(sd, sd))
            res = []
            for b in range(NB):
                res.append(V.did(V.w(tk).tensor_scalar(dst[:, b, :], src[:, b, :], mv[:, b, 0:1], sd[:, b:b + 1],
                                                       ALU.subtract, ALU.mult)))
            return res

        hbuf = [mk(NB, D) for _ in range(2)]
        hT = mk(NB, 2, 128)
        WI = [mk(2, 768) for _ in range(2)]
        whh = mk(2, 768)
        wih = mk(2, 768)
        wt = mk(2, 256)
        brz = mk(512)
        bin_, bhn = mk(256), mk(256)
        bt = mk(512)
        NPAN = 4
        pan = [mk(5, 512) for _ in range(NPAN)]
        s_pan = [new_sem() for _ in range(NPAN)]
        aggT = [mk(2, 512) for _ in range(2)]
        rz = [mk(512) for _ in range(2)]
        nn = [mk(256) for _ in range(2)]
        s_w = new_sem()
        t0 = G.did(G.e.memset(hbuf[0][:, 24, :], 0.0))
        tg = G.did(G.e.memset(hbuf[1][:, 24, :], 0.0))
        s_x = new_sem()
        tx = load_rows(hbuf[0], a["x"], S, s_x, t0)
        load(S, whh[:, :, :], a["w_hhT"].rearrange("(k p) n -> p k n", p=128), s_w)
        load(S, wih[:, :, :], a["w_ihT"].rearrange("(k p) n -> p k n", p=128), s_w)
        load(S, brz, a["b_ih"][0:512].unsqueeze(0).partition_broadcast(128), s_w)
        load(S, bt, a["b_hh"][0:512].unsqueeze(0).partition_broadcast(128), s_w)
        load(S, bin_, a["b_ih"][512:768].unsqueeze(0).partition_broadcast(128), s_w)
        tw = load(S, bhn, a["b_hh"][512:768].unsqueeze(0).partition_broadcast(128), s_w)
        t_b = V.did(V.w(tw).tensor_tensor(brz, brz, bt, ALU.add))
        mark = top[0]
        t_h = layernorm(hbuf[0], hbuf[0], [tx])
        t_hT = {}
        t_ev = {}
        for b in range(NB):
            bank = 6 + b % 2
            T.w(t_h[b], *([t_ev[b - 2]] if b >= 2 else []))
            for f in range(2):
                ins = T.e.transpose(PS[:, bank, f * 128:(f + 1) * 128], hbuf[0][:, b, f * 128:(f + 1) * 128], ident)
            tt = T.did(ins)
            t_ev[b] = t_hT[b] = A.did(A.w(tt).activation(hT[:, b, :, :], PS[:, bank, 0:256].rearrange("p (f n) -> p f n", f=2),
                                                         ACT.Copy))
        s_wt = new_sem()
        npan = 0
        t_pan_free = {}
        t_agg_free = {}
        t_agg_ev = [None] * 2
        tr_use = {6: t_ev[24], 7: t_ev[23]}
        t_rz_free, t_nn_free = {}, {}
        t_WI_free = {}
        gb = 0
        avq = AD.rearrange("(q p n) o -> q p (n o)", q=NG, p=128)
        pend_panels = [(l, q, k) for l in range(5) for q in range(NG) for k in range(5)]
        t_panel = {}
        issued = [0]

        def issue_panel():
            if issued[0] >= len(pend_panels):
                return
            i = issued[0]
            l, q, k = pend_panels[i]
            w = [t_adj] + ([t_pan_free[i - NPAN]] if i >= NPAN else [])
            m = cols_of(q)
            src = avq[q, :, k * 2560:(k + 1) * 2560]
            if m == 512:
                t_panel[i] = load(S, pan[i % NPAN].rearrange("p a b -> p (a b)"), src, s_pan[i % NPAN], *w)
            else:
                t_panel[i] = load(S, pan[i % NPAN][:, :, 0:m], src.rearrange("p (a b) -> p a b", a=5)[:, :, 0:m],
                                  s_pan[i % NPAN], *w)
            issued[0] += 1

        gcount = [0]

        def gru(l, b, ag, t_ag, cur, nxt):
            n = rows_of(b)
            c = (b % 4) * 128
            r = gcount[0] % 2
            gcount[0] += 1
            rzb, nnb, trb = 2 + r, 4 + r, 6 + r
            T.w(t_ag, t_hT[b], t_WI[l], tw, *([t_rz_free[r]] if r in t_rz_free else []),
                *([t_nn_free[r]] if r in t_nn_free else []))
            for (dst, lo, hi, both) in ((PS[0:n, rzb, :], 0, 512, True),):
                for f in range(2):
                    T.e.matmul(dst, lhsT=ag[:, f, c:c + n], rhs=WI[l % 2][:, f, lo:hi], start=(f == 0), stop=False)
                for f in range(2):
                    ins = T.e.matmul(dst, lhsT=hT[:, b, f, 0:n], rhs=whh[:, f, lo:hi], start=False, stop=(f == 1))
            t_rz = T.did(ins)
            for f in range(2):
                T.e.matmul(PS[0:n, nnb, 0:256], lhsT=ag[:, f, c:c + n], rhs=WI[l % 2][:, f, 512:768], start=(f == 0), stop=(f == 1))
            for f in range(2):
                ins = T.e.matmul(PS[0:n, nnb, 256:512], lhsT=hT[:, b, f, 0:n], rhs=whh[:, f, 512:768],
                                 start=(f == 0), stop=(f == 1))
            t_nn = T.did(ins)
            zr, z2, t3 = rz[r][0:n], rz[r][0:n, 256:512], nn[r][0:n]
            t_rz_free[r] = tk = V.did(V.w(t_rz, t_b).tensor_tensor(zr, PS[0:n, rzb, :], brz[0:n], ALU.add))
            t_sg = A.did(A.w(tk).activation(zr, zr, ACT.Sigmoid))
            tk = V.did(V.w(t_nn).tensor_tensor(t3, PS[0:n, nnb, 256:512], bhn[0:n], ALU.add))
            tk = V.did(V.w(tk, t_sg).tensor_tensor(t3, t3, rz[r][0:n, 0:256], ALU.mult))
            t_nn_free[r] = tk = V.did(V.w(tk).tensor_tensor(t3, t3, PS[0:n, nnb, 0:256], ALU.add))
            tk = V.did(V.w(tk).tensor_tensor(t3, t3, bin_[0:n], ALU.add))
            t_th = A.did(A.w(tk).activation(t3, t3, ACT.Tanh))
            h0, h1 = hbuf[cur][0:n, b, :], hbuf[nxt][0:n, b, :]
            tk = V.did(V.w(t_th, tg).tensor_tensor(h1, h0, t3, ALU.subtract))
            tk = V.did(V.w(tk).tensor_tensor(h1, h1, z2, ALU.mult))
            tk = V.did(V.w(tk).tensor_tensor(h1, h1, t3, ALU.add))
            return tk, t_nn, n, trb

        def retranspose(b, n, trb, nxt, t_new, t_old_used):
            T.w(t_new, tr_use[trb])
            for f in range(2):
                ins = T.e.transpose(PS[:, trb, f * 128:f * 128 + n], hbuf[nxt][0:n, b, f * 128:(f + 1) * 128],
                                    ident[0:n, 0:n])
            tt = T.did(ins)
            tr_use[trb] = t_hT[b] = A.did(A.w(tt, t_old_used).activation(
                hT[:, b, :, 0:n], PS[:, trb, 0:256].rearrange("p (f n) -> p f n", f=2)[:, :, 0:n], ACT.Copy))

        t_WI = {}
        t_hnew = {b: t_h[b] for b in range(NB)}
        t_wt_free = None
        lastg = None
        for l in range(5):
            cur, nxt = l % 2, (l + 1) % 2
            w = [t_wt_free] if t_wt_free else []
            twt = load(S, wt[:, :, :], a["weightT"][l].rearrange("(k p) n -> p k n", p=128), s_wt, *w)
            for _ in range(NPAN if l == 0 else 0):
                issue_panel()
            evs = []
            for m in range(2):
                bank = 2 + m
                for (lo, hi, bk) in ((0, 512, 2 + m), (512, 768, 4 + m)):
                    T.w(twt, tw, *([t_rz_free[m], t_nn_free[m]] if m in t_rz_free else []))
                    for k in range(2):
                        ins = T.e.matmul(PS[:, bk, 0:hi - lo], lhsT=wt[:, k, m * 128:(m + 1) * 128], rhs=wih[:, k, lo:hi],
                                         start=(k == 0), stop=(k == 1))
                    tt = T.did(ins)
                    free = [lastg] if lastg else []
                    ev = A.did(A.w(tt, *free).activation(WI[l % 2][:, m, lo:hi], PS[:, bk, 0:hi - lo], ACT.Copy))
                    evs.append(ev)
                t_rz_free[m] = evs[-2]
                t_nn_free[m] = evs[-1]
            t_wt_free = tt
            t_WI[l] = evs[-1]
            agg_done = {}
            queue = []
            pendT = []
            for q in range(NG + 1):
                if q < NG:
                    m = cols_of(q)
                    for k in range(5):
                        i = (l * NG + q) * 5 + k
                        T.w(t_panel[i], *([t_agg_free[0]] if 0 in t_agg_free and k == 0 else []))
                        for s5 in range(5):
                            sb = 5 * k + s5
                            T.w(t_hnew[sb])
                            for f in range(2):
                                ins = T.e.matmul(PS[:, f, 0:m], lhsT=hbuf[cur][:, sb, f * 128:(f + 1) * 128],
                                                 rhs=pan[i % NPAN][:, s5, 0:m], start=(sb == 0), stop=(sb == NB - 1))
                        t_pan_free[i] = T.did(ins)
                        issue_panel()
                    t_mm = t_pan_free[i]
                    ag = aggT[q % 2]
                    w = [t_agg_ev[q % 2]] if t_agg_ev[q % 2] else []
                    e0 = A.did(A.w(t_mm, *w).activation(ag[:, 0, 0:m], PS[:, 0, 0:m], ACT.Copy))
                    e1 = V.did(V.w(t_mm, *w).tensor_copy(ag[:, 1, 0:m], PS[:, 1, 0:m]))
                    agg_done[q] = (e0, e1)
                    t_agg_free[0] = e0
                    T_agg_extra = e1
                if q >= 1:
                    p = q - 1
                    e0, e1 = agg_done[p]
                    T.w(e1)
                    for b in range(4 * p, min(4 * p + 4, NB)):
                        tk, t_nn, n, trb = gru(l, b, aggT[p % 2], e0, cur, nxt)
                        t_hnew[b] = tk
                        lastg = t_nn
                        pendT.append((b, n, trb, nxt, tk, t_nn))
                        if len(pendT) > 1:
                            retranspose(*pendT.pop(0))
                    t_agg_ev[p % 2] = t_nn
                if q < NG:
                    T.w(agg_done[q][1])
            while pendT:
                retranspose(*pendT.pop(0))
        probe("h", hbuf[1])
        if stop <= 4:
            return
        meet()
        top[0] = base_top
        X = mk(NB, D)
        hold = hbuf[1]
        t0 = G.did(G.e.memset(X[:, 24, :], 0.0))
        tx = load_rows(X, a["x"], S, s_x, t0)
        for b in range(NB):
            tX = V.did(V.w(tx).tensor_tensor(X[:, b, :], X[:, b, :], hold[:, b, :], ALU.add))
        probe("x1", X)
        meet()
        x_top = top[0]

        def transpose_rows(Y, b, dstT, bank, *ticks):
            T.w(*ticks)
            for f in range(2):
                ins = T.e.transpose(PS[:, bank, f * 128:(f + 1) * 128], Y[:, b, f * 128:(f + 1) * 128], ident)
            tt = T.did(ins)
            return A.did(A.w(tt).activation(dstT, PS[:, bank, 0:256].rearrange("p (f n) -> p f n", f=2), ACT.Copy))

        Y = mk(NB, D)
        W1 = mk(2, 1024)
        b1c = mk(8)
        Wg = mk(8, 8)
        Wd = mk(8, 2048)
        bg = mk(8)
        bd = mk(256)
        yT = [mk(2, 512) for _ in range(2)]
        HT = [mk(8, 512) for _ in range(1)]
        gt = mk(NB, 8)
        sm = mk(6, 8)
        gT = mk(128)
        s_w = new_sem()
        load(S, W1[:, :, :], a["W1"].rearrange("(k p) n -> p k n", p=128), s_w)
        load(S, b1c, a["b1T"], s_w)
        load(S, Wg[:, :, :], a["Wg"].rearrange("(k p) n -> p k n", p=128), s_w)
        load(S, bg, a["bg"].unsqueeze(0).partition_broadcast(128), s_w)
        load(S, bd[0:8], a["bd"], s_w)
        tw = load(S, Wd[:, :, :].rearrange("p k (e n) -> p k e n", e=8),
                  a["Wd"].rearrange("e (k p) n -> p k e n", p=128), s_w) if False else None
        for e in range(8):
            tw = load(S, Wd[:, :, e * 256:(e + 1) * 256], a["Wd"][e].rearrange("(k p) n -> p k n", p=128), s_w)
        t_y = layernorm(Y, X, [tX])
        t_yt, t_ps, t_ht_free = {}, {}, {}
        free = {i: None for i in range(8)}

        def fw(bank):
            return [free[bank]] if free[bank] else []

        nb_ = 0
        last_exp = None
        for q in range(NG):
            nbk = min(4, NB - 4 * q)
            m = nbk * 128
            for j in range(nbk):
                bank = 6 + j % 2
                b = 4 * q + j
                free[bank] = t_yt = transpose_rows(Y, b, yT[q % 2][:, :, j * 128:(j + 1) * 128], bank, t_y[b], *fw(bank))
            for c in range(8):
                bank = c % 2
                T.w(t_yt, tw, free[6] if free[6] else t_yt, free[7] if free[7] else t_yt, *fw(bank))
                for k in range(2):
                    ins = T.e.matmul(PS[:, bank, 0:m], lhsT=W1[:, k, c * 128:(c + 1) * 128], rhs=yT[q % 2][:, k, 0:m],
                                     start=(k == 0), stop=(k == 1))
                tt = T.did(ins)
                w = [last_exp] if last_exp else []
                free[bank] = t_ht = A.did(A.w(tt, *w).activation(HT[0][:, c, 0:m], PS[:, bank, 0:m], ACT.Gelu, bias=b1c[:, c:c + 1]))
            for j in range(nbk):
                b = 4 * q + j
                cs = slice(j * 128, (j + 1) * 128)
                T.w(t_ht, *fw(6))
                for k in range(8):
                    ins = T.e.matmul(PS[:, 6, 0:8], lhsT=HT[0][:, k, cs], rhs=Wg[:, k, :], start=(k == 0), stop=(k == 7))
                tt = T.did(ins)
                lg, ex, sc = sm[:, 0, :], sm[:, 1, :], sm[:, 2, :]
                mx, sx, g_ = sm[:, 3, 0:1], sm[:, 3, 1:2], gt[:, b, :]
                tk = V.did(V.w(tt).tensor_tensor(lg, PS[:, 6, 0:8], bg, ALU.add))
                free[6] = tk
                tk = V.did(V.w(tk).tensor_reduce(mx, lg, AX, ALU.max, negate=True))
                tk = A.did(A.w(tk).activation(ex, lg, ACT.Exp, bias=mx, accum_out=sx))
                tk = V.did(V.w(tk).reciprocal(sx, sx))
                tk = V.did(V.w(tk).tensor_scalar(ex, ex, sx, None, ALU.mult))
                tk = V.did(V.w(tk).tensor_reduce(mx, ex, AX, ALU.max))
                tk = V.did(V.w(tk).tensor_scalar(lg, ex, mx, None, ALU.is_equal))
                tk = V.did(V.w(tk).tensor_tensor_scan(sc, ones[:, 0:8], lg, 0.0, ALU.mult, ALU.add))
                tk = V.did(V.w(tk).scalar_tensor_tensor(lg, sc, 1.0, lg, ALU.is_equal, ALU.mult))
                t_g = V.did(V.w(tk).tensor_scalar(g_, lg, mx, None, ALU.mult))
                for p in range(4):
                    bank = 2 + p
                    T.w(*fw(bank))
                    for k in range(8):
                        ins = T.e.matmul(PS[:, bank, :], lhsT=HT[0][:, k, cs], rhs=Wd[:, k, p * 512:(p + 1) * 512],
                                         start=(k == 0), stop=(k == 7))
                    tt = last_exp = T.did(ins)
                    V.w(tt, t_g)
                    for e in (2 * p, 2 * p + 1):
                        V.w(*([tX] if tX else []))
                        free[bank] = tX = V.did(V.e.scalar_tensor_tensor(
                            X[:, b, :], PS[:, bank, (e % 2) * 256:(e % 2) * 256 + 256], gt[:, b, e:e + 1], X[:, b, :],
                            ALU.mult, ALU.add))
                tt = T.did(T.w(t_g, *fw(7)).transpose(PS[0:8, 7, 0:128], g_, ident))
                tk = A.did(A.w(tt).activation(gT[0:8], PS[0:8, 7, 0:128], ACT.Copy))
                tt = T.did(T.w(tk).matmul(PS[:, 7, 0:256], lhsT=gT[0:8], rhs=bd[0:8], start=True, stop=True))
                free[7] = tX = V.did(V.w(tt, tX).tensor_tensor(X[:, b, :], X[:, b, :], PS[:, 7, 0:256], ALU.add))
        probe("x2", X)
        if stop <= 5:
            return
        meet()
        top[0] = x_top

        lin = mk(52, 16, 8)

        def tiles(x, t, n):
            return x[:, t % 52:t % 52 + n, t // 52, :]

        sl = mk(T2)
        idxS, idxD = mk(T2, dt=I32), mk(T2, dt=I32)
        gat_top = top[0]
        Y = mk(NB, D)
        Wa = mk(2, 256)
        av5 = mk(5, 256)
        yT = [mk(2, 128) for _ in range(2)]
        row = [mk(272) for _ in range(2)]
        u1 = mk(256)
        u2 = mk(256)
        s_w = new_sem()
        load(S, Wa[:, :, :], a["Wgat"].rearrange("(k p) n -> p k n", p=128), s_w)
        tw = load(S, av5.rearrange("p a b -> p (a b)"), a["a5"].rearrange("a b -> (a b)").unsqueeze(0).partition_broadcast(128), s_w)
        t_y = layernorm(Y, X, [tX])
        cS, cD, a5h = av5[:, 0, :], av5[:, 1, :], av5[:, 4, :]
        V.did(V.w(tw).tensor_tensor(cS, cS, av5[:, 2, :], ALU.subtract))
        V.did(V.e.tensor_tensor(cD, cD, av5[:, 2, :], ALU.add))
        t_c = V.did(V.e.tensor_scalar(a5h, a5h, 0.5, None, ALU.mult))
        fs = u1
        ia = mk(T2, dt=I32)
        fa = mk(T2)
        tk = V.did(V.e.tensor_copy(fa, srcc))
        bl2 = bc(blkf.unsqueeze(2), [128, T2 // 2, 2])
        tk = V.did(V.w(tk).scalar_tensor_tensor(sl.rearrange("p (a b) -> p a b", b=2), bl2, -128.0,
                                                fa.rearrange("p (a b) -> p a b", b=2), ALU.mult, ALU.add))
        tk = V.did(V.e.tensor_scalar(fa, fa, float(N - 1), None, ALU.min))
        tk = V.did(V.w(tk).tensor_copy(idxS, fa))
        tk = V.did(V.w(tk).tensor_copy(fa, dstc))
        tk = V.did(V.w(tk).tensor_scalar(fa, fa, float(N - 1), None, ALU.min))
        t_ix = V.did(V.w(tk).tensor_copy(idxD, fa))
        tk = V.did(V.w(tk).tensor_scalar(blkf, blkf, 264.0, None, ALU.mult))
        t_blko = V.did(V.w(tk).tensor_copy(blko, blkf))
        s_row = [new_sem(), new_sem()]
        t_row = {}
        ev = {}
        mmt = {}
        for b in range(NB):
            r = b % 2
            ty = transpose_rows(Y, b, yT[r], 6 + r, t_y[b], *([ev[b - 2], mmt[b - 2]] if b >= 2 else []))
            ev[b] = ty
            T.w(ty, tw, *([ev2[b - 2]] if b >= 2 else []))
            if b == 0:
                ev2 = {}
            for k in range(2):
                ins = T.e.matmul(PS[:, r, 0:256], lhsT=yT[r][:, k, :], rhs=Wa[:, k, :], start=(k == 0), stop=(k == 1))
            mmt[b] = T.did(ins)
            w = [t_row[b - 2], t_n2[b - 2]] if b >= 2 else []
            if b == 0:
                t_n2 = {}
            ev2[b] = A.did(A.w(mmt[b], *w).activation(row[r][:, 0:256], PS[:, r, 0:256], ACT.Copy))
            hr = row[r][:, 0:256]
            tk = V.did(V.w(ev2[b], t_c).tensor_tensor(u1, hr, a5h, ALU.mult))
            t2 = V.did(V.w(tk).tensor_tensor(u2, u1, cS, ALU.add))
            t2 = V.did(V.w(t2).tensor_tensor(u2, u2, hr, ALU.mult))
            t2 = V.did(V.w(t2).tensor_reduce(row[r][:, 256:264], u2.rearrange("p (h d) -> p h d", h=8), AX, ALU.add))
            t3 = V.did(V.w(t2).tensor_tensor(u2, u1, cD, ALU.add))
            t3 = V.did(V.w(t3).tensor_tensor(u2, u2, hr, ALU.mult))
            t_n2[b] = V.did(V.w(t3).tensor_reduce(row[r][:, 264:272], u2.rearrange("p (h d) -> p h d", h=8), AX, ALU.add))
            t_row[b] = load(S, HD[b * 128:(b + 1) * 128, :], row[r], s_row[r], t_n2[b], ev2[b])
        t_hd = [t_row[23], t_row[24]]
        probe("sl", sl)
        meet(*t_hd)
        top[0] = gat_top
        A4 = mk(2, 8)
        A5 = mk(2, 8)
        NR = 3
        Sg = [mk(4, 272) for _ in range(NR)]
        Dg = [mk(4, 272) for _ in range(NR)]
        df = [mk(4, 256) for _ in range(2)]
        ab = [mk(8, 128) for _ in range(2)]
        sq = [mk(8, 128) for _ in range(2)]
        msk = mk(2, 8)
        s_w = new_sem()
        a45 = mk(4)
        load(S, a45[:, 0:2], a["a4c"], s_w)
        load(S, a45[:, 2:4], a["a5c"], s_w)
        tw = load(S, msk[:, :, :], a["c_mask"], s_w)
        V.w(tw)
        tk = V.did(V.e.tensor_scalar(a45[:, 2:4], a45[:, 2:4], -0.5, None, ALU.mult))
        V.w(tk)
        for f in range(2):
            V.did(V.e.tensor_scalar(A4[:, f, :], msk[:, f, :], a45[:, f:f + 1], None, ALU.mult))
            t_a = V.did(V.e.tensor_scalar(A5[:, f, :], msk[:, f, :], a45[:, 2 + f:3 + f], None, ALU.mult))
        s_g = [new_sem() for _ in range(NR)]
        t_df, t_tr, t_sq, t_ab, t_mm, t_lin = {}, {}, {}, {}, {}, {}
        NQ = T2 // 4

        def gat_reduce(i):
            r = i % 2
            T.w(t_ab[i], t_sq[i], t_a, *([t_lin[i - 2]] if i >= 2 else []))
            for j in range(4):
                for k, (src_, co) in enumerate(((ab[r], A4), (ab[r], A4), (sq[r], A5), (sq[r], A5))):
                    f = k % 2
                    ins = T.e.matmul(PS[:, 4 + r, j * 8:(j + 1) * 8], lhsT=src_[:, 2 * j + f, :], rhs=co[:, f, :],
                                     start=(k == 0), stop=(k == 3))
            t_mm[i] = T.did(ins)
            sg, dg = Sg[i % NR], Dg[i % NR]
            ln = tiles(lin, 4 * i, 4)
            tk = V.did(V.w(t_mm[i]).tensor_tensor(ln, PS[:, 4 + r, 0:32].rearrange("p (j h) -> p j h", h=8),
                                                 sg[:, :, 256:264], ALU.add))
            t_lin[i] = V.did(V.w(tk).tensor_tensor(ln, ln, dg[:, :, 264:272], ALU.add))

        for i in range(NQ + 1):
            if i < NQ:
                r = i % 2
                n = i % NR
                G.w(t_ix, *t_hd, *([t_lin[i - NR], t_df[i - NR]] if i >= NR else []))
                for j in range(4):
                    t = 4 * i + j
                    for buf, ix in ((Sg[n], idxS), (Dg[n], idxD)):
                        tg_ = s_g[n].add(G.e.indirect_dma_start(buf[:, j, :], None, HD[:, :],
                                                                bass.IndirectOffsetOnAxis(ap=ix[:, t:t + 1], axis=0)), 16)
                t_df[i] = V.did(V.w(tg_, *([t_tr[i - 2]] if i >= 2 else [])).tensor_tensor(
                    df[r], Dg[n][:, :, 0:256], Sg[n][:, :, 0:256], ALU.subtract))
                T.w(t_df[i], *([t_ab[i - 2], t_sq[i - 2]] if i >= 2 else []))
                for j in range(4):
                    for f in range(2):
                        k = 2 * j + f
                        ins = T.e.transpose(PS[:, 2 * r + k // 4, (k % 4) * 128:(k % 4 + 1) * 128],
                                            df[r][:, j, f * 128:(f + 1) * 128], ident)
                t_tr[i] = T.did(ins)
                pv = PS[:, 2 * r:2 * r + 2, :]
                A.w(t_tr[i], *([t_mm[i - 2]] if i >= 2 else []))
                t_ab[i] = A.did(A.e.activation(ab[r].rearrange("p (b k) n -> p b (k n)", b=2), pv, ACT.Abs))
                t_sq[i] = A.did(A.e.activation(sq[r].rearrange("p (b k) n -> p b (k n)", b=2), pv, ACT.Square))
            if i >= 1:
                gat_reduce(i - 1)
        probe("lin", lin)
        if stop <= 6:
            return
        meet()
        top[0] = gat_top
        L = 52 * 128
        AT = mk(L)
        PEN = mk(L + 1)
        SR = mk(L)
        srb = mk(52, 16, 8)
        sm4 = mk(4)
        q8 = mk(16, 4)
        lk = mk(4, 16)
        cc = mk(1)
        al = lin
        t_al = V.did(V.e.scalar_tensor_tensor(al, lin, 0.2, lin, ALU.mult, ALU.max))
        t_sb = V.did(V.e.tensor_copy(srb, bc(srcc.rearrange("p (a g) -> p g a", g=52).unsqueeze(3), [128, 52, 16, 8])))
        alv = al.rearrange("p g a h -> p g (a h)")
        srv = srb.rearrange("p g a h -> p g (a h)")
        ev = {}
        for k in range(13):
            for n, (v, dst, eng) in enumerate(((alv, AT, A), (srv, SR, V))):
                bank = 2 * (k % 2) + n
                T.w(t_al, t_sb, *([ev[(k - 2, n)]] if k >= 2 else []))
                for j in range(4):
                    ins = T.e.transpose(PS[:, bank, j * 128:(j + 1) * 128], v[:, 4 * k + j, :], ident)
                tt = T.did(ins)
                o = dst[:, 512 * k:512 * (k + 1)]
                if n == 0:
                    ev[(k, n)] = A.did(A.w(tt).activation(o, PS[:, bank, :], ACT.Copy))
                else:
                    ev[(k, n)] = V.did(V.w(tt).tensor_copy(o, PS[:, bank, :]))
        t_at, t_sr = ev[(12, 0)], ev[(12, 1)]
        V.did(V.w(t_sr).memset(PEN[:, 0:1], -BIG))
        V.did(V.e.memset(PEN[:, L:L + 1], -BIG))
        tk = V.did(V.e.tensor_tensor(PEN[:, 1:L], SR[:, 1:L], SR[:, 0:L - 1], ALU.not_equal))
        t_pen = V.did(V.w(tk).tensor_scalar(PEN[:, 1:L], PEN[:, 1:L], -BIG, None, ALU.mult))
        V.did(V.w(t_pen).tensor_reduce(sm4[:, 1:2], PEN[:, 1:L], AX, ALU.min))
        V.did(V.e.tensor_copy(sm4[:, 2:3], SR[:, 0:1]))
        V.did(V.e.tensor_copy(sm4[:, 3:4], SR[:, L - 1:L]))
        tk = V.did(V.w(t_pen, t_at).tensor_tensor_scan(AT, PEN[:, 0:L], AT, -BIG, ALU.add, ALU.max))
        tk = V.did(V.w(tk).tensor_copy(sm4[:, 0:1], AT[:, L - 1:L]))
        s_q = [new_sem() for _ in range(6)]
        tk = load(S, Q1[:, :], sm4, s_q[0], tk)
        tk = load(S, q8[0:8, :, :], Q1.rearrange("(a h) f -> h a f", h=8), s_q[1], tk)
        link, ch = lk[0:8, 0, :], lk[0:8, 1, :]
        xs, cr = lk[0:8, 2, :], lk[0:8, 3, :]
        V.did(V.w(tk).memset(link[:, 0:1], -BIG))
        tk = V.did(V.e.tensor_tensor(link[:, 1:16], q8[0:8, 1:16, 2], q8[0:8, 0:15, 3], ALU.not_equal))
        tk = V.did(V.w(tk).tensor_scalar(link[:, 1:16], link[:, 1:16], -BIG, None, ALU.mult))
        tk = V.did(V.w(tk).tensor_tensor(ch, link, q8[0:8, :, 1], ALU.min))
        tk = V.did(V.w(tk).tensor_tensor_scan(xs, ch, q8[0:8, :, 0], -BIG, ALU.add, ALU.max))
        V.did(V.e.memset(cr[:, 0:1], -BIG))
        tk = V.did(V.w(tk).tensor_tensor(cr[:, 1:16], xs[:, 0:15], link[:, 1:16], ALU.add))
        tk = load(S, Q2.rearrange("(a h) f -> h (a f)", h=8), cr, s_q[2], tk, allow_slow_non_contiguous=True)
        tk = load(S, cc, Q2[:, :], s_q[3], tk)
        tk = V.did(V.w(tk).tensor_tensor(AT[:, 0:1], AT[:, 0:1], cc, ALU.max))
        tk = V.did(V.w(tk).tensor_tensor_scan(AT, PEN[:, 0:L], AT, -BIG, ALU.add, ALU.max))
        rA, rP = AT[:, ::-1], PEN[:, 1:L + 1][:, ::-1]
        tk = V.did(V.w(tk).tensor_tensor_scan(rA, rP, rA, -BIG, ALU.add, ALU.max))
        tk = load(S, Q3[:, :], AT[:, 0:1], s_q[4], tk)
        tk = load(S, q8[0:8, :, 0:1], Q3.rearrange("(a h) f -> h a f", h=8), s_q[5], tk, allow_slow_non_contiguous=True)
        V.did(V.w(tk).memset(ch[:, 15:16], -BIG))
        tk = V.did(V.e.tensor_tensor(ch[:, 0:15], link[:, 1:16], q8[0:8, 0:15, 1], ALU.min))
        tk = V.did(V.w(tk).tensor_tensor_scan(xs[:, ::-1], ch[:, ::-1], q8[0:8, :, 0][:, ::-1], -BIG, ALU.add, ALU.max))
        V.did(V.e.memset(cr[:, 15:16], -BIG))
        tk = V.did(V.w(tk).tensor_tensor(cr[:, 0:15], xs[:, 1:16], link[:, 1:16], ALU.add))
        s_q2 = [new_sem(), new_sem()]
        tk = load(S, Q4.rearrange("(a h) f -> h (a f)", h=8), cr, s_q2[0], tk, allow_slow_non_contiguous=True)
        tk = load(S, cc, Q4[:, :], s_q2[1], tk)
        tk = V.did(V.w(tk).tensor_tensor(AT[:, L - 1:L], AT[:, L - 1:L], cc, ALU.max))
        t_mx = V.did(V.w(tk).tensor_tensor_scan(rA, rP, rA, -BIG, ALU.add, ALU.max))
        ev = {}
        for k in range(13):
            bank = k % 4
            T.w(t_mx, *([ev[k - 4]] if k >= 4 else []))
            for j in range(4):
                g = 4 * k + j
                ins = T.e.transpose(PS[:, bank, j * 128:(j + 1) * 128], AT[:, g * 128:(g + 1) * 128], ident)
            tt = T.did(ins)
            o = alv[:, 4 * k:4 * k + 4, :]
            ev[k] = V.did(V.w(tt).tensor_tensor(o, o, PS[:, bank, :].rearrange("p (g m) -> p g m", g=4), ALU.subtract))
        lv = lin.rearrange("p g a h -> p (g a h)")
        t_e = A.did(A.w(ev[12]).activation(lv, lv, ACT.Exp))
        probe("ex", lin)
        meet()
        top[0] = gat_top
        acc = mk(NB, 264)
        NR = 6
        Dg = [mk(2, 272) for _ in range(NR)]
        Wv = [mk(2, 264) for _ in range(3)]
        On = [mk(2, 128) for _ in range(3)]
        s_g = [new_sem() for _ in range(NR)]
        regs = [nc.vector.alloc_register(f"blk{i}") for i in range(8)]
        accf = acc.rearrange("p b n -> p (b n)")
        t_acc = V.did(V.e.memset(accf, 0.0))
        t_wv, t_on, t_mm, t_ce, t_ac = {}, {}, {}, {}, {}
        for i in range(NPAIR + 1):
            if i < NPAIR:
                n, r = i % NR, i % 3
                G.w(*([t_wv[i - NR]] if i >= NR else []))
                for j in range(2):
                    t = 2 * i + j
                    tg_ = s_g[n].add(G.e.indirect_dma_start(Dg[n][:, j, :], None, HD[:, :],
                                                            bass.IndirectOffsetOnAxis(ap=idxD[:, t:t + 1], axis=0)), 16)
                free3 = [t_mm[i - 3]] if i >= 3 else []
                ee = tiles(lin, 2 * i, 2)
                t_ce[i] = A.did(A.w(t_e, *free3).activation(Wv[r][:, :, 256:264], ee, ACT.Copy))
                V.w(t_e, *free3)
                for j in range(2):
                    t_on[i] = V.did(V.e.tensor_scalar(On[r][:, j, :], iota, sl[:, 2 * i + j:2 * i + j + 1], None, ALU.is_equal))
                t_wv[i] = V.did(V.w(tg_).tensor_tensor(
                    Wv[r][:, :, 0:256].rearrange("p j (h d) -> p j h d", h=8),
                    Dg[n][:, :, 0:256].rearrange("p j (h d) -> p j h d", h=8),
                    bc(ee.unsqueeze(3), [128, 2, 8, 32]), ALU.mult))
                T.w(t_wv[i], t_on[i], t_ce[i], *([t_ac[i - 3]] if i >= 3 else []))
                for j in range(2):
                    ins = T.e.matmul(PS[:, r, 0:264], lhsT=On[r][:, j, :], rhs=Wv[r][:, j, :], start=(j == 0), stop=(j == 1))
                t_mm[i] = T.did(ins)
            if i >= 1:
                p = i - 1
                if p % 8 == 0:
                    V.e.reg_load(regs[0:min(8, NPAIR - p)], blko[0:1, p:p + min(8, NPAIR - p)])
                v = V.e.snap(regs[p % 8], min_val=0, max_val=24 * 264)
                dst = accf[:, bass.ds(v, 264)]
                t_acc = t_ac[p] = V.did(V.w(t_acc, t_mm[p]).tensor_tensor(dst, dst, PS[:, p % 3, 0:264], ALU.add))
        sd = acc[:, :, 256:264]
        tk = V.did(V.w(t_acc).tensor_scalar(sd, sd, 1.0e-16, None, ALU.add))
        tk = V.did(V.w(tk).reciprocal(sd, sd))
        o4 = acc[:, :, 0:256].rearrange("p b (h d) -> p b h d", h=8)
        for b in range(NB):
            t1 = V.did(V.w(tk).tensor_tensor(o4[:, b], o4[:, b], bc(sd[:, b].unsqueeze(2), [128, 8, 32]), ALU.mult))
            tX = V.did(V.w(t1).tensor_tensor(X[:, b, :], X[:, b, :], acc[:, b, 0:256], ALU.add))
        probe("x3", X)
        if stop <= 7:
            return
        meet()
        top[0] = x_top

        Y = mk(NB, D)
        yT = mk(2, NB * 128)
        gt = mk(NB, 16)
        gw = mk(2, 16)
        gbb = mk(16)
        b1c = mk(16, 4)
        b2 = mk(256)
        gT = mk(128)
        W1 = [mk(2, 512) for _ in range(2)]
        W2 = [mk(4, 256) for _ in range(2)]
        HT = [mk(4, 512) for _ in range(2)]
        s_w = new_sem()
        load(S, gw[:, :, :], a["gate_w"].rearrange("(k p) n -> p k n", p=128), s_w)
        load(S, gbb, a["gate_b"].unsqueeze(0).partition_broadcast(128), s_w)
        load(S, b1c[:, :, :], a["b1m"], s_w)
        tw = load(S, b2[0:16], a["b2"], s_w)
        s_e = [new_sem(), new_sem()]
        t_we = {}
        t_efree = {}

        def load_expert(e):
            w = [t_efree[e - 2]] if e >= 2 else []
            load(S, W1[e % 2][:, :, :], a["w1"][e].rearrange("(k p) n -> p k n", p=128), s_e[e % 2], *w)
            t_we[e] = load(S, W2[e % 2][:, :, :], a["w2"][e].rearrange("(k p) n -> p k n", p=128), s_e[e % 2])

        load_expert(0)
        load_expert(1)
        mark = top[0]
        t_y = layernorm(Y, X, [tX])
        lgt = mk(NB, 16)
        s1, s2 = mk(NB, 16), mk(NB, 16)
        mm = mk(4, NB)
        rst = mk(NB, 16)
        free = {i: None for i in range(8)}
        for b in range(NB):
            bank = 6 + b % 2
            free[bank] = ty = transpose_rows(Y, b, yT[:, :, b * 128:(b + 1) * 128], bank, t_y[b], *fw(bank))
            bank = b % 2
            T.w(ty, tw, *fw(bank))
            for k in range(2):
                ins = T.e.matmul(PS[:, bank, 0:16], lhsT=yT[:, k, b * 128:(b + 1) * 128], rhs=gw[:, k, :],
                                 start=(k == 0), stop=(k == 1))
            tt = T.did(ins)
            free[bank] = t_lg = V.did(V.w(tt).tensor_tensor(lgt[:, b, :], PS[:, bank, 0:16], gbb, ALU.add))
        m1, m2, ew, wa = (mm[:, i, :] for i in range(4))

        def first_max(dst, val, mx, tk):
            t0 = V.did(V.e.memset(rst, 1.0))
            t0 = V.did(V.w(t0).memset(rst[:, :, 0:1], 0.0))
            tk = V.did(V.w(tk, t0).tensor_tensor(dst, val, bc(mx.unsqueeze(2), [128, NB, 16]), ALU.is_equal))
            tk = V.did(V.w(tk).tensor_tensor_scan(s2.rearrange("p b e -> p (b e)"), rst.rearrange("p b e -> p (b e)"),
                                                  dst.rearrange("p b e -> p (b e)"), 0.0, ALU.mult, ALU.add))
            return V.did(V.w(tk).scalar_tensor_tensor(dst, s2, 1.0, dst, ALU.is_equal, ALU.mult))

        tk = V.did(V.w(t_lg).tensor_reduce(m1, lgt, AX, ALU.max))
        tk = first_max(s1, lgt, m1, tk)
        tk = V.did(V.w(tk).scalar_tensor_tensor(lgt, s1, -3.0e38, lgt, ALU.mult, ALU.add))
        tk = V.did(V.w(tk).tensor_reduce(m2, lgt, AX, ALU.max))
        tk = first_max(gt, lgt, m2, tk)
        tk = V.did(V.w(tk).tensor_tensor(ew, m2, m1, ALU.subtract))
        tk = A.did(A.w(tk).activation(ew, ew, ACT.Exp))
        tk = V.did(V.w(tk).tensor_scalar(wa, ew, 1.0, None, ALU.add))
        tk = V.did(V.w(tk).reciprocal(wa, wa))
        tk = V.did(V.w(tk).tensor_tensor(ew, ew, wa, ALU.mult))
        t1 = V.did(V.w(tk).tensor_tensor(s1, s1, bc(wa.unsqueeze(2), [128, NB, 16]), ALU.mult))
        t2 = V.did(V.w(tk).tensor_tensor(gt, gt, bc(ew.unsqueeze(2), [128, NB, 16]), ALU.mult))
        t_gt = V.did(V.w(t1, t2).tensor_tensor(gt, gt, s1, ALU.add))
        t_yy = {b: None for b in range(NB)}
        for b in range(NB):
            tt = T.did(T.w(t_gt, *fw(7)).transpose(PS[0:16, 7, 0:128], gt[:, b, :], ident))
            tk = A.did(A.w(tt).activation(gT[0:16], PS[0:16, 7, 0:128], ACT.Copy))
            tt = T.did(T.w(tk, *fw(b % 2)).matmul(PS[:, b % 2, 0:256], lhsT=gT[0:16], rhs=b2[0:16], start=True, stop=True))
            free[7] = tk
            free[b % 2] = t_yy[b] = V.did(V.w(tt).tensor_tensor(Y[:, b, :], Y[:, b, :], PS[:, b % 2, 0:256], ALU.add))
        fb_ = {i: t_yy[24] for i in range(8)}
        ht_free = {}
        units = [(e, q) for e in range(16) for q in range(NG)]
        t_ht = {}
        nmm2 = [0]
        for u in range(len(units) + 1):
            if u < len(units):
                e, q = units[u]
                m = min(512, (NB - 4 * q) * 128)
                if q == 0 and 2 <= e + 1 < 16:
                    pass
                T.w(t_we[e])
                for c in range(4):
                    T.w(fb_[c])
                    for k in range(2):
                        ins = T.e.matmul(PS[:, c, 0:m], lhsT=W1[e % 2][:, k, c * 128:(c + 1) * 128],
                                         rhs=yT[:, k, 512 * q:512 * q + m], start=(k == 0), stop=(k == 1))
                    tt = T.did(ins)
                    w = [ht_free[u - 2]] if u >= 2 else []
                    fb_[c] = t_ht[u] = A.did(A.w(tt, *w).activation(HT[u % 2][:, c, 0:m], PS[:, c, 0:m], ACT.Relu,
                                                                    bias=b1c[:, e, c:c + 1]))
            if u >= 1:
                e, q = units[u - 1]
                T.w(t_ht[u - 1])
                for b in range(4 * q, min(4 * q + 4, NB)):
                    bank = 4 + nmm2[0] % 4
                    nmm2[0] += 1
                    T.w(fb_[bank])
                    cs = slice((b % 4) * 128, (b % 4) * 128 + 128)
                    for k in range(4):
                        ins = T.e.matmul(PS[:, bank, 0:256], lhsT=HT[(u - 1) % 2][:, k, cs], rhs=W2[e % 2][:, k, :],
                                         start=(k == 0), stop=(k == 3))
                    tt = T.did(ins)
                    fb_[bank] = t_yy[b] = V.did(V.w(tt, t_yy[b]).scalar_tensor_tensor(
                        Y[:, b, :], PS[:, bank, 0:256], gt[:, b, e:e + 1], Y[:, b, :], ALU.mult, ALU.add))
                ht_free[u - 1] = tt
                if q == NG - 1:
                    t_efree[e] = tt
                    if e + 2 < 16:
                        load_expert(e + 2)
        meet()
        probe("y", Y)
        top[0] = mark
        gm, bt = mk(256), mk(256)
        load(S, gm, a["gamma"].unsqueeze(0).partition_broadcast(128), s_w)
        tw = load(S, bt, a["beta"].unsqueeze(0).partition_broadcast(128), s_w)
        t_y = layernorm(Y, Y, [t_yy[24]])
        V.w(tw)
        s_o = new_sem()
        tks = []
        for b in range(NB):
            tk = V.did(V.w(t_y[b]).tensor_tensor(Y[:, b, :], Y[:, b, :], gm, ALU.mult))
            tk = V.did(V.w(tk).tensor_tensor(Y[:, b, :], Y[:, b, :], bt, ALU.add))
            tks.append(V.did(V.w(tk).tensor_tensor(Y[:, b, :], Y[:, b, :], X[:, b, :], ALU.add)))
        load(S, out[0:3072, :].rearrange("(b p) d -> p b d", p=128), Y[:, 0:24, :], s_o, tks[-1])
        tk = load(S, out[3072:N, :], Y[0:TAIL, 24, :], s_o)
        S.w(tk)


def constants():
    e = np.arange(128)
    sq = np.zeros((128, 5, 128), np.float32)
    sq[:, 0] = np.eye(128)
    sq[:, 1] = e[None, :]
    sq[:, 2] = e[None, :] < e[:, None]
    sq[:, 3] = e[:, None] < e[None, :]
    sq[:, 4] = 1.0
    mask = np.zeros((128, 2, 8), np.float32)
    for f in range(2):
        for p in range(128):
            mask[p, f, (f * 128 + p) // 32] = 1.0
    return {
        "c_sq": sq,
        "c_pairs": np.tile(np.arange(T2 // 2, dtype=np.float32)[None, :], (128, 1)),
        "c_pidx": e.astype(np.float32)[:, None],
        "c_eps": np.full((128, 1), 1e-5, np.float32),
        "c_mask": mask,
    }


def arrays_of(i):
    c = np.ascontiguousarray
    g = {k: np.asarray(v) for k, v in i.items()}
    w = g["L1_gnn_a"].reshape(8, 5, 32)
    r = {
        "x": g["x"], "src": g["src"], "dst": g["dst"], "edge_weight": g["edge_weight"],
        "weightT": g["L0_gnn_weight"].transpose(0, 2, 1), "w_ihT": g["L0_gnn_w_ih"].T, "w_hhT": g["L0_gnn_w_hh"].T,
        "b_ih": g["L0_gnn_b_ih"], "b_hh": g["L0_gnn_b_hh"],
        "W1": g["L0_ffn_W1"], "b1T": g["L0_ffn_b1"].reshape(8, 128).T, "Wg": g["L0_ffn_Wg"], "bg": g["L0_ffn_bg"],
        "Wd": g["L0_ffn_Wd"], "bd": g["L0_ffn_bd"],
        "Wgat": g["L1_gnn_W"].transpose(1, 0, 2).reshape(256, 256),
        "a5": w.transpose(1, 0, 2).reshape(5, 256),
        "a4c": w[:, 3].reshape(2, 128).T, "a5c": w[:, 4].reshape(2, 128).T,
        "gate_w": g["L1_ffn_gate_w"], "gate_b": g["L1_ffn_gate_b"], "w1": g["L1_ffn_w1"],
        "b1m": g["L1_ffn_b1"].reshape(16, 4, 128).transpose(2, 0, 1), "w2": g["L1_ffn_w2"], "b2": g["L1_ffn_b2"],
        "gamma": g["L1_ffn_gamma"], "beta": g["L1_ffn_beta"],
    }
    return {k: c(v) for k, v in r.items()} | constants()


def kernel(**inputs):
    import concourse.bacc as bacc
    from concourse.bass_utils import run_bass_kernel_spmd

    nc = bacc.Bacc("TRN2", target_bir_lowering=False, num_devices=1)
    arrays = arrays_of(inputs)
    aps = {k: nc.dram_tensor(k, v.shape, mybir.dt.from_np(v.dtype), kind="ExternalInput").ap() for k, v in arrays.items()}
    out = nc.dram_tensor("out", (N, D), F32, kind="ExternalOutput").ap()
    program(nc, aps, out)
    r = run_bass_kernel_spmd(nc, [arrays], core_ids=[0])
    return r.results[0]["out"]
```

```python
import numpy as np
import concourse.bass as bass
from concourse import mybir
from contextlib import ExitStack

F32 = mybir.dt.float32
I32 = mybir.dt.int32
BF = mybir.dt.bfloat16
ALU = mybir.AluOpType
ACT = mybir.ActivationFunctionType
AX = mybir.AxisListType.X

N = 3125
NB = 25
TAIL = N - 24 * 128
D = 256
E = 100000
T1 = 782
T2 = 832
NPAIR = 415
PADKEY = 8000
NG = 7
AROW = NB * 512
ASIZE = NG * 128 * AROW
BIG = 1.0e30
NT0 = 32
NT1 = 64


class Sem:
    def __init__(self, handle):
        self.handle = handle
        self.n = 0

    def add(self, ins, k):
        ins.then_inc(self.handle, k)
        self.n += k
        return self, self.n


class Eng:

    def __init__(self, e, new_sem):
        self.e = e
        self.new_sem = new_sem
        self.sem = new_sem()
        self.seen = {}

    def w(self, *ticks):
        for s, v in ticks:
            if self.seen.get(s, 0) < v:
                self.e.wait_ge(s.handle, v)
                self.seen[s] = v
        return self.e

    def did(self, ins):
        if self.sem.n >= 20000:
            self.sem = self.new_sem()
        return self.sem.add(ins, 1)

    def last(self):
        return [(self.sem, self.sem.n)] if self.sem.n else []


def program(nc, a, out):
    ctx = ExitStack()
    with ctx:
        names = [0]

        def new_sem():
            names[0] += 1
            return Sem(ctx.enter_context(nc.semaphore(f"s{names[0]}")))

        V, A, T, G, S = (Eng(e, new_sem) for e in (nc.vector, nc.scalar, nc.tensor, nc.gpsimd, nc.sync))
        engines = (V, A, T, G, S)
        MEMW = 52800
        mem = ctx.enter_context(nc.sbuf_tensor("mem", [128, MEMW], F32))
        PS = ctx.enter_context(nc.psum_tensor("PS", [128, 8, 512], F32))
        top = [0]

        def mk(*dims, dt=F32):
            n = 1
            for d in dims:
                n *= d
            words = n if dt != BF else (n + 1) // 2
            o = top[0]
            top[0] += words
            assert top[0] <= MEMW, top[0] * 4
            v = mem[:, o:o + words]
            if dt != F32:
                v = v.bitcast(dt)
            if dt == BF and n % 2:
                v = v[:, 0:n]
            if len(dims) == 2:
                v = v.rearrange("p (a b) -> p a b", a=dims[0])
            if len(dims) == 3:
                v = v.rearrange("p (a b c) -> p a b c", a=dims[0], b=dims[1])
            return v

        def dram(name, shape, dt):
            return nc.dram_tensor(name, shape, dt, kind="Internal").ap()

        def load(q, dst, src, sem, *ticks, **kw):
            return sem.add(q.w(*ticks).dma_start(dst, src, **kw), 16)

        def meet(*ticks):
            ends = [t for g in engines for t in g.last()] + list(ticks)
            for g in engines:
                g.w(*ends)

        def bc(ap, shape):
            return ap.broadcast_to(shape)

        SA = dram("sorted_by_dst", (128 * T1, 4), I32)
        SB = dram("sorted_by_src", (128 * T2, 4), I32)
        AD = dram("adjacency", (ASIZE, 1), F32)
        HD = dram("gat_rows", (NB * 128, 272), F32)
        SPL = dram("gathered_rows", (T2 // 4, 128, 1024), F32)
        XSR = dram("moe_in", (NT1 * 128, D), F32)
        YSR = dram("moe_out", (NT1 * 128, D), F32)
        HR = dram("hidden_rows", (NB * 128, 1024), F32)
        TI = dram("slot_token", (128 * NT0, 1), I32)
        YS0 = dram("expert_rows", (NT0 * 128, D), F32)
        XD = dram("x_kept", (128, NB * D), F32)
        Q1 = dram("carry_in", (128, 4), F32)
        Q2 = dram("carry_fwd", (128, 1), F32)
        Q3 = dram("carry_mid", (128, 1), F32)
        Q4 = dram("carry_bwd", (128, 1), F32)

        cst = mk(5, 128)
        ident, iota, lowt, upt, ones = (cst[:, i, :] for i in range(5))
        pidx = mk(1)
        epsc = mk(1)
        tailc = mk(1)
        tokid = mk(NB, dt=I32)
        pairs = mk(T2 // 2)
        identb = mk(128, dt=BF)
        iotab = mk(128, dt=BF)
        rec_top = top[0]
        recB = mk(T2, 4, dt=I32)
        blko = mk(T2 // 2, dt=I32)
        blkf = mk(T2 // 2)
        base_top = top[0]

        s_c = new_sem()
        load(S, cst[:, :, :], a["c_sq"], s_c)
        load(S, pairs, a["c_pairs"], s_c)
        load(S, pidx, a["c_pidx"], s_c)
        load(S, tailc, a["c_tail"], s_c)
        load(S, tokid, a["c_tok"], s_c)
        tc = load(S, epsc, a["c_eps"], s_c)
        V.did(V.w(tc).tensor_copy(identb, ident))
        tk = V.did(V.e.tensor_copy(iotab, iota))
        for g in engines:
            g.w(tc, tk)

        padt = recB
        zt = mk(1600)
        tz = G.did(G.e.memset(zt, 0.0))
        tp = G.did(G.e.memset(padt[:, :, 2:4], 0))
        tp = G.did(G.w(tp).memset(padt[:, :, 0:2], PADKEY))
        s_pad = new_sem()
        t_pad = load(G, SB.rearrange("(p t) f -> p (t f)", p=128), padt[:, :, :].rearrange("p t f -> p (t f)"), s_pad, tp)
        def route(OH, C, nE, NT, tk):
            pc = mk(C, nE)
            tot2 = mk(nE, C)
            cum = mk(nE, C)
            ts, pt, ex, st = (mk(nE) for _ in range(4))
            pi = mk(nE, dt=I32)
            pos = mk(C)
            posi = mk(C, dt=I32)
            eid = mk(NT)
            n = C * nE
            oh = OH.rearrange("p c e -> p (c e)")
            T.w(tk)
            for lo in range(0, n, 512):
                hi = min(lo + 512, n)
                T.e.matmul(PS[:, lo // 512, 0:hi - lo], lhsT=upt, rhs=oh[:, lo:hi], start=True, stop=True)
                ins = T.e.matmul(PS[:, 2 + lo // 512, 0:hi - lo], lhsT=ones, rhs=oh[:, lo:hi], start=True, stop=True)
            tt = T.did(ins)
            P1 = PS[:, 0:2, :].rearrange("p b n -> p (b n)")[:, 0:n]
            P2 = PS[:, 2:4, :].rearrange("p b n -> p (b n)")[:, 0:n].rearrange("p (c e) -> p e c", e=nE)
            tk = V.did(V.w(tt).tensor_copy(tot2, P2))
            t0 = V.did(V.w(tk).tensor_reduce(ts, tot2, AX, ALU.add))
            t1 = V.did(V.e.tensor_tensor_scan(cum.rearrange("p e c -> p (e c)"), bc(ones[:, 0:1], [128, n]),
                                              tot2.rearrange("p e c -> p (e c)"), 0.0, ALU.mult, ALU.add))
            tk = V.did(V.w(t0).tensor_scalar(pt, ts, 127.0, None, ALU.add))
            tk = V.did(V.w(tk).tensor_copy(pi, pt))
            tk = V.did(V.w(tk).tensor_single_scalar(pi, pi, 7, ALU.logical_shift_right))
            tk = V.did(V.w(tk).tensor_copy(pt, pi))
            tk = V.did(V.w(tk).tensor_tensor_scan(st, ones[:, 0:nE], pt, 0.0, ALU.mult, ALU.add))
            t2 = V.did(V.e.tensor_tensor_scan(ex, ones[:, 0:nE], ts, 0.0, ALU.mult, ALU.add))
            tk = V.did(V.w(tk).tensor_tensor(st, st, pt, ALU.subtract))
            t2 = V.did(V.w(t2).tensor_tensor(ex, ex, ts, ALU.subtract))
            te = V.did(V.w(tk).tensor_scalar(eid, pairs[:, 0:NT], st[:, 1:2], None, ALU.is_ge))
            for e in range(2, nE):
                te = V.did(V.w(te).scalar_tensor_tensor(eid, pairs[:, 0:NT], st[:, e:e + 1], eid, ALU.is_ge, ALU.add))
            tk = V.did(V.w(tk, t2).scalar_tensor_tensor(ex, st, 128.0, ex, ALU.mult, ALU.subtract))
            t1 = V.did(V.w(t1).tensor_tensor(cum, cum, tot2, ALU.subtract))
            t1 = V.did(V.w(t1, tk).tensor_tensor(cum, cum, bc(ex.unsqueeze(2), [128, nE, C]), ALU.add))
            t1 = V.did(V.w(t1).tensor_tensor(pc, P1.rearrange("p (c e) -> p c e", e=nE),
                                             cum.rearrange("p e c -> p c e"), ALU.add))
            t1 = V.did(V.w(t1).tensor_tensor(pc, pc, OH, ALU.mult))
            t1 = V.did(V.w(t1).tensor_reduce(pos, pc, AX, ALU.add))
            t1 = V.did(V.w(t1).tensor_copy(posi, pos))
            return pos, posi, t1, eid, te

        def sort(P, NC, rec, kc, t_rec, dest, TT, drop, aligned):
            mark = top[0]
            tmpi = mk(NC, dt=I32)
            keyf = mk(NC)
            lob, hib, h128 = (mk(NC, dt=BF) for _ in range(3))
            Ohi = mk(NC, 25, dt=BF)
            H = mk(25, NC + 1)
            olo = top[0]
            Olo = [mk(20, 128, dt=BF) for _ in range(5)]
            tot = mk(25)
            toti = mk(25, dt=I32)
            inc = mk(25)
            off = mk(25)
            key = rec[:P, :, kc]
            V.did(V.w(t_rec).tensor_copy(keyf[:P], key))
            tk = V.did(V.e.tensor_single_scalar(tmpi[:P], key, 127, ALU.bitwise_and))
            tk = V.did(V.w(tk).tensor_copy(lob[:P], tmpi[:P]))
            tk = V.did(V.w(tk).tensor_single_scalar(tmpi[:P], key, 7, ALU.logical_shift_right))
            tk = V.did(V.w(tk).tensor_copy(hib[:P], tmpi[:P]))
            tk = V.did(V.w(tk).tensor_scalar(h128[:P], tmpi[:P], 128.0, None, ALU.mult))
            t_ohis = []
            t_ohis.append(V.did(V.w(tk).tensor_tensor(
                Ohi[:P], bc(hib[:P].unsqueeze(2), [P, NC, 25]),
                bc(iotab[:P, 0:25].unsqueeze(1), [P, NC, 25]), ALU.is_equal)))
            groups = [(c, min(20, NC - c)) for c in range(0, NC, 20)]
            t_mm, t_ev, user = {}, {}, {}
            T.w(*t_ohis)
            for g, (c0, n) in enumerate(groups):
                k = 3 + g // 3 % 2 if g % 3 == 1 else (g - g // 3 - (g % 3 == 2)) % 3
                ol = Olo[k][:P, 0:n, :]
                w = [t_mm[user[k]]] if k in user else []
                user[k] = g
                sides = (bc(lob[:P, c0:c0 + n].unsqueeze(2), [P, n, 128]), bc(iotab[:P].unsqueeze(1), [P, n, 128]))
                if g % 3 == 1:
                    t_ol = G.did(G.w(tk, *w).tensor_tensor(ol, *sides, ALU.subtract))
                    t_ol = A.did(A.w(t_ol).activation(ol, ol, ACT.Square))
                    t_ol = A.did(A.w(t_ol).activation(ol, ol, ACT.Relu, bias=ones[:P, 0:1], scale=-1.0))
                else:
                    t_ol = V.did(V.w(tk, *w).tensor_tensor(ol, *sides, ALU.is_equal))
                T.w(t_ol, *([t_ev[g - 2]] if g >= 2 else []))
                for j in range(n):
                    T.e.matmul(PS[:, 4, 0:25], lhsT=ol[:, j, :], rhs=Ohi[:P, c0 + j, :],
                               start=(c0 + j == 0), stop=(c0 + j == NC - 1))
                    ins = T.e.matmul(PS[:, g % 2, j * 25:(j + 1) * 25], lhsT=ol[:, j, :],
                                     rhs=Ohi[:P, c0 + j, :], start=True, stop=True)
                t_mm[g] = T.did(ins)
                t_ev[g] = A.did(A.w(t_mm[g]).activation(
                    H[:, :, 1 + c0:1 + c0 + n],
                    PS[:, g % 2, 0:n * 25].rearrange("p (j b) -> p b j", b=25), ACT.Copy))
            tk = V.did(V.w(t_mm[len(groups) - 1]).tensor_copy(tot, PS[:, 4, 0:25]))
            T.w(tk).matmul(PS[:, 2, 0:25], lhsT=upt, rhs=tot, start=True, stop=True)
            t_tot = T.did(T.e.matmul(PS[:, 3, 0:25], lhsT=ones, rhs=tot, start=True, stop=True))
            if aligned:
                tk = V.did(V.w(t_tot).tensor_scalar(tot, PS[:, 3, 0:25], 255.0, None, ALU.add))
                tk = V.did(V.w(tk).tensor_copy(toti, tot))
                tk = V.did(V.w(tk).tensor_single_scalar(toti, toti, 8, ALU.logical_shift_right))
                tk = V.did(V.w(tk).tensor_copy(tot, toti))
                tk = V.did(V.w(tk).tensor_scalar(tot, tot, 256.0, None, ALU.mult))
            else:
                tk = V.did(V.w(t_tot).tensor_copy(tot, PS[:, 3, 0:25]))
            tk = V.did(V.w(tk).tensor_tensor_scan(inc, ones[:, 0:25], tot, 0.0, ALU.mult, ALU.add))
            V.w(t_ev[len(groups) - 1], t_ev[len(groups) - 2])
            tk = V.did(V.w(tk).tensor_tensor(inc, inc, tot, ALU.subtract))
            tk = t_inc = V.did(V.w(tk).tensor_tensor(off, inc, PS[:, 2, 0:25], ALU.add))
            for b in range(25):
                V.did(V.w(tk).tensor_copy(H[:, b, 0:1], off[:, b:b + 1]))
                t_scan = V.did(V.e.tensor_tensor_scan(H[:, b, 1:NC + 1], bc(ones[:, 0:1], [128, NC]), H[:, b, 1:NC + 1],
                                                      off[:, b:b + 1], ALU.mult, ALU.add))
            if aligned:
                tk = V.did(V.w(t_inc).tensor_scalar(inc, inc, 1.0 / 256.0, None, ALU.mult))
                tk = V.did(V.w(tk).tensor_scalar(blkf, pairs, inc[:, 1:2], None, ALU.is_ge))
                for b in range(2, 25):
                    tk = V.did(V.w(tk).scalar_tensor_tensor(blkf, pairs, inc[:, b:b + 1], blkf, ALU.is_ge, ALU.add))
            top_h = top[0]
            OT = [mem[:, olo + 512 * i:olo + 512 * (i + 1)].rearrange("p (a b) -> p a b", a=4) for i in range(2)]
            R = mk(NC)
            B = mk(NC)
            junk = [mk(128) for _ in range(4)]
            t_jk = {}
            tmp = mem[:, olo + 1280:olo + 1780].rearrange("p (a b) -> p a b", a=20)
            posi = mk(NC, dt=I32)
            rowi = tmpi
            padf = mk(NC) if drop else None
            if drop:
                tk = V.did(V.w(t_rec).tensor_scalar(padf[:P], keyf[:P], 4000.0, 1.0e6, ALU.is_ge, ALU.mult))
                t_padf = tk
            nsub = (NC + 3) // 4
            t_lr, t_kr, t_ot, t_rk, t_bs, t_cmb = {}, {}, {}, {}, {}, {}
            s_scat = new_sem()
            t_idx_done = None

            def cols(s):
                return range(4 * s, min(4 * s + 4, NC))

            def base(s):
                T.w(t_ot[s], t_scan)
                for c in cols(s):
                    g, j = c // 20, c % 20
                    if j == 0 and g >= 2:
                        T.w(t_cmb[g - 2])
                    ins = T.e.matmul(PS[:P, 4 + g % 2, j * 25:(j + 1) * 25], lhsT=OT[s % 2][:, c % 4, 0:P],
                                     rhs=H[:, :, c], start=True, stop=True)
                t_bs[s] = T.did(ins)

            def finish(c0, c1):
                w = slice(c0, c1)
                tk = V.did(V.w(t_rk[(c1 - 1) // 4], t_cmb[(c1 - 1) // 20]).tensor_tensor(
                    B[:P, w], B[:P, w], R[:P, w], ALU.add))
                tk = V.did(V.w(tk).tensor_copy(posi[:P, w], B[:P, w]))
                V.did(V.w(tk).tensor_single_scalar(rowi[:P, w], posi[:P, w], 127, ALU.bitwise_and))
                tk = V.did(V.e.tensor_single_scalar(posi[:P, w], posi[:P, w], 7, ALU.logical_shift_right))
                tk = V.did(V.w(tk).tensor_copy(B[:P, w], rowi[:P, w]))
                tk = V.did(V.w(tk).tensor_copy(R[:P, w], posi[:P, w]))
                tk = V.did(V.w(tk).scalar_tensor_tensor(B[:P, w], B[:P, w], float(TT), R[:P, w], ALU.mult, ALU.add))
                if drop:
                    tk = V.did(V.w(tk).tensor_tensor(B[:P, w], B[:P, w], padf[:P, w], ALU.add))
                tk = V.did(V.w(tk).tensor_copy(rowi[:P, w], B[:P, w]))
                G.w(tk, t_pad)
                for c in range(c0, c1):
                    r = s_scat.add(G.e.indirect_dma_start(
                        dest[:, :], bass.IndirectOffsetOnAxis(ap=rowi[:P, c:c + 1], axis=0), rec[:P, c, :], None,
                        bounds_check=128 * TT - 1, oob_is_err=False), 16)
                return r

            done = 0
            for s in range(nsub + 1):
                if s < nsub:
                    T.w(*([t_ot[s - 2], t_rk[s - 2]] if s >= 2 else [t_tot, t_inc]))
                    for c in cols(s):
                        j = c % 4
                        lo = bc(lob[:P, c:c + 1], [P, 128])
                        hi = bc(h128[:P, c:c + 1], [P, 128])
                        T.e.matmul(PS[:, s % 2, j * 128:j * 128 + P], lhsT=lo, rhs=identb[:P, :P], start=True, stop=True)
                        T.e.matmul(PS[:, 2 + s % 2, j * 128:j * 128 + P], lhsT=hi, rhs=identb[:P, :P], start=True, stop=False)
                        ins = T.e.matmul(PS[:, 2 + s % 2, j * 128:j * 128 + P], lhsT=lo, rhs=identb[:P, :P],
                                         start=False, stop=True)
                    t_lr[s] = T.did(ins)
                    n = len(cols(s))
                    lr = PS[:, s % 2, 0:n * 128].rearrange("p (j e) -> p j e", e=128)[:, :, 0:P]
                    t_ot[s] = V.did(V.w(t_lr[s], *([t_bs[s - 2]] if s >= 2 else [])).tensor_scalar(
                        OT[s % 2][:, 0:n, 0:P], lr, pidx, None, ALU.is_equal))
                    for c in cols(s):
                        j = c % 4
                        t_rk[s] = t_jk[c] = V.did(V.w(*([t_jk[c - 4]] if c >= 4 else [])).scalar_tensor_tensor(
                            junk[j][:P, 0:P], PS[:P, 2 + s % 2, j * 128:j * 128 + P], keyf[:P, c:c + 1],
                            lowt[:P, 0:P], ALU.is_equal, ALU.mult, accum_out=R[:P, c:c + 1]))
                if s >= 1:
                    base(s - 1)
                    c1 = min(4 * s, NC)
                    if c1 % 20 == 0 or c1 == NC:
                        g = (c1 - 1) // 20
                        c0, n = groups[g]
                        tk = V.did(V.w(t_bs[s - 1], *([t_cmb[g - 1]] if g else [])).tensor_tensor(
                            tmp[:P, 0:n, :], PS[:P, 4 + g % 2, 0:n * 25].rearrange("p (j b) -> p j b", b=25),
                            Ohi[:P, c0:c0 + n, :], ALU.mult))
                        t_cmb[g] = V.did(V.w(tk).tensor_reduce(B[:P, c0:c0 + n], tmp[:P, 0:n, :], AX, ALU.add))
                        if c1 - done >= (100 if done >= 300 else 20) or c1 == NC:
                            t_all = finish(done, c1)
                            done = c1
            top[0] = mark
            return t_all

        hi_mem = mem[:, MEMW - 2400:MEMW]
        rec0 = mk(800, 4, dt=I32)
        rec1 = rec0[:, 0:T1, :]
        flag = mk(1, dt=I32)
        lists_top = top[0]
        tab = mk(2, T1, dt=I32)
        nxt = mk(T1, dt=I32)
        wgt = mk(T1)
        cur, later = mk(T1), mk(T1)
        desc = mk(1)
        s_in = new_sem()
        load(S, tab[:, 1, :], a["dstP"], s_in)
        load(S, nxt, a["nextP"], s_in)
        load(S, tab[:, 0, :], a["srcP"], s_in)
        ti = load(S, wgt, a["wP"], s_in)
        s_zero = new_sem()
        av = AD.rearrange("(k p n) o -> k p (n o)", p=128, n=1600)
        for k in range(ASIZE // (128 * 1600)):
            t_zero = load(A, av[k], zt, s_zero, tz, ti)

        xz = XSR.rearrange("(k p m) d -> k p (m d)", p=128, m=4)
        for k in range(NT1 // 4):
            t_zero = load(A, xz[k], zt[:, 0:1024], s_zero)
        t_zero = load(A, TI.rearrange("(p t) o -> p (t o)", p=128), zt[:, 0:NT0].bitcast(I32), s_zero)

        t1 = V.did(V.w(ti).tensor_copy(cur, tab[:, 1, :]))
        t2 = V.did(V.e.tensor_copy(later, nxt))
        tk = V.did(V.w(t1, t2).tensor_tensor(cur, cur, later, ALU.is_gt))
        tk = V.did(V.w(tk).tensor_reduce(desc, cur, AX, ALU.add))
        tk = T.did(T.w(tk).matmul(PS[:, 7, 0:1], lhsT=ones, rhs=desc, start=True, stop=True))
        t_flag = V.did(V.w(tk).tensor_copy(flag, PS[:, 7, 0:1]))
        V.did(V.e.memset(rec1[:, :, 3:4], 0))
        V.did(V.e.tensor_copy(rec1[:, :, 0], tab[:, 0, :]))
        V.did(V.e.tensor_copy(rec1[:, :, 1], tab[:, 1, :]))
        t_rec1 = V.did(V.e.tensor_copy(rec1[:, :, 2].bitcast(F32), wgt))
        unsorted = nc.alloc_registers("unsorted")
        for g in engines:
            g.w(t_flag)
        nc.regs_load(unsorted, flag[0:1, 0:1])
        outer = [(g.sem, dict(g.seen)) for g in engines]
        with nc.If_ne(unsorted, 0):
            meet(t_rec1, t_pad)
            for g in engines:
                g.sem = new_sem()
            top[0] = lists_top
            s_in = new_sem()
            ts = load(S, SA.rearrange("(p t) f -> p (t f)", p=128),
                      padt[:, 0:T1, :].rearrange("p t f -> p (t f)"), s_in)
            srt, drt = hi_mem[:, 0:800].bitcast(I32), hi_mem[:, 800:1600].bitcast(I32)
            wrt = hi_mem[:, 1600:2400]
            load(S, srt[:125], a["src"].rearrange("(p c) -> p c", p=125), s_in)
            load(S, drt[:125], a["dst"].rearrange("(p c) -> p c", p=125), s_in)
            ti = load(S, wrt[:125], a["edge_weight"].rearrange("(p c) -> p c", p=125), s_in)
            V.did(V.w(ti).memset(rec0[:125, :, 3:4], 0))
            V.did(V.e.tensor_copy(rec0[:125, :, 0], srt[:125]))
            V.did(V.e.tensor_copy(rec0[:125, :, 1], drt[:125]))
            tr = V.did(V.e.tensor_copy(rec0[:125, :, 2].bitcast(F32), wrt[:125]))
            G.w(ti)
            tall = sort(125, 800, rec0[:125], 1, tr, SA, T1, False, False)
            meet(tall)
            ti = load(S, rec1.rearrange("p t f -> p (t f)"), SA.rearrange("(p t) f -> p (t f)", p=128), s_in)
            meet(ti)
        for g, (sem, seen) in zip(engines, outer):
            g.sem, g.seen = sem, seen
        top[0] = lists_top
        ti = t_rec1
        s_in2 = new_sem()
        tall = sort(128, T1, rec1, 0, ti, SB, T2, True, True)
        meet(tall, t_zero)
        top[0] = base_top
        t_rec = load(S, recB.rearrange("p t f -> p (t f)"), SB.rearrange("(p t) f -> p (t f)", p=128), s_in2)

        SF = mk(T2)
        NLF = mk(T2)
        aidx = mk(T2, dt=I32)
        keep_top = top[0]
        hbuf = [mk(NB, D) for _ in range(2)]
        hT = mk(NB, 2, 128)
        WI = [mk(2, 768) for _ in range(2)]
        whh = mk(2, 768)
        wih = mk(2, 768)
        wt = mk(2, 256)
        brz = mk(512)
        bin_, bhn = mk(256), mk(256)
        bt = mk(512)
        NPAN = 4
        pan_at = top[0]
        pan = [mk(5, 512) for _ in range(NPAN)]
        aggT = [mk(2, 512) for _ in range(2)]
        rz = [mk(512) for _ in range(2)]
        nn = [mk(256) for _ in range(2)]
        l0_top = top[0]
        top[0] = pan_at
        ia, ib = mk(T2, dt=I32), mk(T2, dt=I32)
        fa, fb, keyf = mk(T2), mk(T2), mk(T2)
        KT = mk(1026)
        WT = mk(1024)
        EQ = mk(1025)
        SX = mk(1024)
        rows = mk(6, 104)
        cinc = mk(1)
        aone = mk(1)
        assert top[0] <= pan_at + NPAN * 2560
        top[0] = l0_top
        srcc, dstc, wc = recB[:, :, 0], recB[:, :, 1], recB[:, :, 2].bitcast(F32)
        tk = V.did(V.w(t_rec).tensor_copy(fa, srcc))
        tk2 = V.did(V.e.tensor_copy(fb, dstc))
        tk = V.did(V.w(tk, tk2).scalar_tensor_tensor(keyf, fa, 4096.0, fb, ALU.mult, ALU.add))
        kv = keyf.rearrange("p (a g) -> p g a", g=8)
        wv = recB[:, :, 2].bitcast(F32).rearrange("p (a g) -> p g a", g=8)
        T.w(tk, t_rec)
        for g in range(8):
            T.e.transpose(PS[0:104, g // 4, (g % 4) * 128:(g % 4) * 128 + 128], kv[:, g, :], ident)
            ins = T.e.transpose(PS[0:104, 2 + g // 4, (g % 4) * 128:(g % 4) * 128 + 128], wv[:, g, :], ident)
        tt = T.did(ins)
        ta = A.did(A.w(tt).activation(KT[0:104, 1:1025].rearrange("p (b n) -> p b n", b=2), PS[0:104, 0:2, :], ACT.Copy))
        tb = V.did(V.w(tt).tensor_copy(WT[0:104].rearrange("p (b n) -> p b n", b=2), PS[0:104, 2:4, :]))
        T.w(ta).transpose(PS[0:1, 4, 0:104], KT[0:104, 1:2], ident[0:104, 0:104])
        tt = T.did(T.e.transpose(PS[0:1, 4, 128:232], KT[0:104, 1024:1025], ident[0:104, 0:104]))
        t0 = V.did(V.e.memset(rows[0:1, :, :], -1.0))
        V.did(V.w(tt, t0).tensor_copy(rows[0:1, 0, 1:104], PS[0:1, 4, 128:231]))
        tk = V.did(V.e.tensor_copy(rows[0:1, 1, 0:103], PS[0:1, 4, 1:104]))
        T.w(tk).transpose(PS[0:104, 5, 0:1], rows[0:1, 0, :], ident[0:1, 0:1])
        tt = T.did(T.e.transpose(PS[0:104, 5, 1:2], rows[0:1, 1, :], ident[0:1, 0:1]))
        V.did(V.w(tt, ta).tensor_copy(KT[0:104, 0:1], PS[0:104, 5, 0:1]))
        tk = V.did(V.e.tensor_copy(KT[0:104, 1025:1026], PS[0:104, 5, 1:2]))
        tk = V.did(V.w(tk).tensor_tensor(EQ[0:104], KT[0:104, 1:1026], KT[0:104, 0:1025], ALU.is_equal))
        t1 = V.did(V.w(tk, tb).tensor_tensor_scan(SX[0:104], EQ[0:104, 0:1024], WT[0:104], 0.0, ALU.mult, ALU.add))
        t2 = V.did(V.e.tensor_reduce(aone[0:104], EQ[0:104, 1:1024], AX, ALU.min))
        T.w(t1, t2).transpose(PS[0:1, 6, 0:104], SX[0:104, 1023:1024], ident[0:104, 0:104])
        T.e.transpose(PS[0:1, 6, 128:232], aone[0:104], ident[0:104, 0:104])
        tt = T.did(T.e.transpose(PS[0:1, 6, 256:360], EQ[0:104, 0:1], ident[0:104, 0:104]))
        V.did(V.w(tt).tensor_copy(rows[0:1, 2, :], PS[0:1, 6, 0:104]))
        tk = V.did(V.e.tensor_copy(rows[0:1, 3, :], PS[0:1, 6, 128:232]))
        tk = V.did(V.w(tk).tensor_tensor(rows[0:1, 3, :], rows[0:1, 3, :], PS[0:1, 6, 256:360], ALU.mult))
        tk = V.did(V.w(tk).tensor_tensor_scan(rows[0:1, 4, :], rows[0:1, 3, :], rows[0:1, 2, :], 0.0, ALU.mult, ALU.add))
        tk0 = V.did(V.e.memset(rows[0:1, 5, 0:1], 0.0))
        tk = V.did(V.w(tk, tk0).tensor_copy(rows[0:1, 5, 1:104], rows[0:1, 4, 0:103]))
        tt = T.did(T.w(tk).transpose(PS[0:104, 5, 2:3], rows[0:1, 5, :], ident[0:1, 0:1]))
        tk = V.did(V.w(tt).tensor_copy(cinc[0:104], PS[0:104, 5, 2:3]))
        tk = V.did(V.w(tk).tensor_tensor_scan(SX[0:104], EQ[0:104, 0:1024], WT[0:104], cinc[0:104], ALU.mult, ALU.add))
        T.w(tk)
        for g in range(8):
            T.e.transpose(PS[:, g // 4, (g % 4) * 128:(g % 4) * 128 + 104], SX[0:104, g * 128:(g + 1) * 128], ident[0:104, 0:104])
            ins = T.e.transpose(PS[:, 2 + g // 4, (g % 4) * 128:(g % 4) * 128 + 104],
                                EQ[0:104, 1 + g * 128:1 + (g + 1) * 128], ident[0:104, 0:104])
        tt = T.did(ins)

        def back(bank):
            return PS[:, bank, :].rearrange("p (g a) -> p g a", g=4)[:, :, 0:104]

        sfv = SF.rearrange("p (a g) -> p g a", g=8)
        nlv = NLF.rearrange("p (a g) -> p g a", g=8)
        for h in range(2):
            t_sf = A.did(A.w(tt).activation(sfv[:, 4 * h:4 * h + 4, :], back(h), ACT.Copy))
            t_nl = V.did(V.w(tt).tensor_copy(nlv[:, 4 * h:4 * h + 4, :], back(2 + h)))
        tk = V.did(V.e.tensor_single_scalar(ia, srcc, 127, ALU.bitwise_and))
        t2 = V.did(V.e.tensor_single_scalar(ib, srcc, 7, ALU.logical_shift_right))
        tk = V.did(V.w(tk).tensor_copy(fa, ia))
        t2 = V.did(V.w(t2).tensor_copy(fb, ib))
        tk = V.did(V.w(tk, t2).tensor_scalar(fa, fa, float(AROW), None, ALU.mult))
        tk = V.did(V.w(tk).scalar_tensor_tensor(fa, fb, 512.0, fa, ALU.mult, ALU.add))
        V.did(V.w(tk).tensor_single_scalar(ia, dstc, 511, ALU.bitwise_and))
        t2 = V.did(V.e.tensor_single_scalar(ib, dstc, 9, ALU.logical_shift_right))
        t2 = V.did(V.w(t2).tensor_copy(fb, ib))
        tk = V.did(V.w(t2).scalar_tensor_tensor(fa, fb, float(128 * AROW), fa, ALU.mult, ALU.add))
        t2 = V.did(V.w(tk).tensor_copy(fb, ia))
        tk = V.did(V.w(t2).tensor_tensor(fa, fa, fb, ALU.add))
        tk = V.did(V.w(tk, t_nl).scalar_tensor_tensor(fa, NLF, 16777216.0, fa, ALU.mult, ALU.add))
        tk = V.did(V.w(tk).tensor_copy(aidx, fa))
        meet()
        s_adj = new_sem()
        for t in range(2 * NPAIR):
            t_adj = s_adj.add(G.e.indirect_dma_start(
                AD[:, :], bass.IndirectOffsetOnAxis(ap=aidx[:, t:t + 1], axis=0), SF[:, t:t + 1], None,
                bounds_check=ASIZE - 1, oob_is_err=False), 16)

        def rows_of(b):
            return TAIL if b == NB - 1 else 128

        def cols_of(q):
            return (TAIL + 3) // 4 * 4 if q == NG - 1 else 512

        def load_rows(dst, src, q, sem, *ticks):
            load(q, dst[:, 0:24, :], src[0:3072, :].rearrange("(b p) d -> p b d", p=128), sem, *ticks)
            return load(q, dst[0:TAIL, 24, :], src[3072:N, :], sem)

        def layernorm(dst, src, t_src):
            st = mk(NB, 6)
            mv = mk(NB, 2)
            sd = mk(NB)
            nb = mk(NB)
            ticks = {}
            for b in range(NB):
                ticks[b] = V.did(V.w(*t_src).bn_stats(st[:, b, :], src[:, b, :]))
            for b in range(NB):
                tk = V.did(V.w(ticks[b]).bn_aggr(mv[:, b, :], st[:, b, :]))
            tk = A.did(A.w(tk).activation(sd, mv[:, :, 1], ACT.Sqrt, bias=epsc))
            tk = V.did(V.w(tk).reciprocal(sd, sd))
            t_nb = V.did(V.w(tk).scalar_tensor_tensor(nb, mv[:, :, 0], -1.0, sd, ALU.mult, ALU.mult))
            res = []
            for b in range(NB):
                if b % 5 in (1, 3):
                    res.append(A.did(A.w(t_nb).activation(dst[:, b, :], src[:, b, :], ACT.Identity,
                                                          bias=nb[:, b:b + 1], scale=sd[:, b:b + 1])))
                else:
                    res.append(V.did(V.w(tk).tensor_scalar(dst[:, b, :], src[:, b, :], mv[:, b, 0:1], sd[:, b:b + 1],
                                                           ALU.subtract, ALU.mult)))
            return res

        s_pan = [new_sem() for _ in range(NPAN)]
        s_w = new_sem()
        t0 = V.did(V.e.memset(hbuf[0][:, 24, :], 0.0))
        tg = V.did(V.e.memset(hbuf[1][:, 24, :], 0.0))
        s_x = new_sem()
        tx = load_rows(hbuf[0], a["x"], S, s_x, t0)
        load(S, whh[:, :, :], a["w_hhT"].rearrange("(k p) n -> p k n", p=128), s_w)
        load(S, wih[:, :, :], a["w_ihT"].rearrange("(k p) n -> p k n", p=128), s_w)
        load(S, brz, a["b_ih"][0:512].unsqueeze(0).partition_broadcast(128), s_w)
        load(S, bt, a["b_hh"][0:512].unsqueeze(0).partition_broadcast(128), s_w)
        load(S, bin_, a["b_ih"][512:768].unsqueeze(0).partition_broadcast(128), s_w)
        tw = load(S, bhn, a["b_hh"][512:768].unsqueeze(0).partition_broadcast(128), s_w)
        t_b = V.did(V.w(tw).tensor_tensor(brz, brz, bt, ALU.add))
        mark = top[0]
        t_h = layernorm(hbuf[0], hbuf[0], [tx])
        t_hT = {}
        t_ev = {}
        for b in range(NB):
            bank = 6 + b % 2
            T.w(t_h[b], *([t_ev[b - 2]] if b >= 2 else []))
            for f in range(2):
                ins = T.e.transpose(PS[:, bank, f * 128:(f + 1) * 128], hbuf[0][:, b, f * 128:(f + 1) * 128], ident)
            tt = T.did(ins)
            t_ev[b] = t_hT[b] = A.did(A.w(tt).activation(hT[:, b, :, :], PS[:, bank, 0:256].rearrange("p (f n) -> p f n", f=2),
                                                         ACT.Copy))
        s_wt = new_sem()
        npan = 0
        t_pan_free = {}
        t_agg_free = {}
        t_agg_ev = [None] * 2
        tr_use = {6: t_ev[24], 7: t_ev[23]}
        t_rz_free, t_nn_free = {}, {}
        t_WI_free = {}
        gb = 0
        avq = AD.rearrange("(q p n) o -> q p (n o)", q=NG, p=128)
        pend_panels = [(l, q, k) for l in range(5) for q in range(NG) for k in range(5)]
        t_panel = {}
        issued = [0]

        def issue_panel():
            if issued[0] >= len(pend_panels):
                return
            i = issued[0]
            l, q, k = pend_panels[i]
            w = [t_adj] + ([t_pan_free[i - NPAN]] if i >= NPAN else [])
            m = cols_of(q)
            src = avq[q, :, k * 2560:(k + 1) * 2560]
            if m == 512:
                t_panel[i] = load(S, pan[i % NPAN].rearrange("p a b -> p (a b)"), src, s_pan[i % NPAN], *w)
            else:
                t_panel[i] = load(S, pan[i % NPAN][:, :, 0:m], src.rearrange("p (a b) -> p a b", a=5)[:, :, 0:m],
                                  s_pan[i % NPAN], *w)
            issued[0] += 1

        gcount = [0]

        def gru(l, b, ag, t_ag, cur, nxt):
            n = rows_of(b)
            c = (b % 4) * 128
            r = gcount[0] % 2
            gcount[0] += 1
            rzb, nnb, trb = 2 + r, 4 + r, 6 + r
            T.w(t_ag, t_hT[b], t_WI[l], tw, *([t_rz_free[r]] if r in t_rz_free else []),
                *([t_nn_free[r]] if r in t_nn_free else []))
            for (dst, lo, hi, both) in ((PS[0:n, rzb, :], 0, 512, True),):
                for f in range(2):
                    T.e.matmul(dst, lhsT=ag[:, f, c:c + n], rhs=WI[l % 2][:, f, lo:hi], start=(f == 0), stop=False)
                for f in range(2):
                    ins = T.e.matmul(dst, lhsT=hT[:, b, f, 0:n], rhs=whh[:, f, lo:hi], start=False, stop=(f == 1))
            t_rz = T.did(ins)
            for f in range(2):
                T.e.matmul(PS[0:n, nnb, 0:256], lhsT=ag[:, f, c:c + n], rhs=WI[l % 2][:, f, 512:768], start=(f == 0), stop=(f == 1))
            for f in range(2):
                ins = T.e.matmul(PS[0:n, nnb, 256:512], lhsT=hT[:, b, f, 0:n], rhs=whh[:, f, 512:768],
                                 start=(f == 0), stop=(f == 1))
            t_nn = T.did(ins)
            zr, z2, t3 = rz[r][0:n], rz[r][0:n, 256:512], nn[r][0:n]
            t_rz_free[r] = tk = V.did(V.w(t_rz, t_b).tensor_tensor(zr, PS[0:n, rzb, :], brz[0:n], ALU.add))
            t_sg = A.did(A.w(tk).activation(zr, zr, ACT.Sigmoid))
            tk = V.did(V.w(t_nn).tensor_tensor(t3, PS[0:n, nnb, 256:512], bhn[0:n], ALU.add))
            tk = V.did(V.w(tk, t_sg).tensor_tensor(t3, t3, rz[r][0:n, 0:256], ALU.mult))
            t_nn_free[r] = tk = V.did(V.w(tk).tensor_tensor(t3, t3, PS[0:n, nnb, 0:256], ALU.add))
            tk = V.did(V.w(tk).tensor_tensor(t3, t3, bin_[0:n], ALU.add))
            t_th = A.did(A.w(tk).activation(t3, t3, ACT.Tanh))
            h0, h1 = hbuf[cur][0:n, b, :], hbuf[nxt][0:n, b, :]
            tk = V.did(V.w(t_th, tg).tensor_tensor(h1, h0, t3, ALU.subtract))
            tk = V.did(V.w(tk).tensor_tensor(h1, h1, z2, ALU.mult))
            tk = V.did(V.w(tk).tensor_tensor(h1, h1, t3, ALU.add))
            return tk, t_nn, n, trb

        def retranspose(b, n, trb, nxt, t_new, t_old_used):
            T.w(t_new, tr_use[trb])
            for f in range(2):
                ins = T.e.transpose(PS[:, trb, f * 128:f * 128 + n], hbuf[nxt][0:n, b, f * 128:(f + 1) * 128],
                                    ident[0:n, 0:n])
            tt = T.did(ins)
            tr_use[trb] = t_hT[b] = A.did(A.w(tt, t_old_used).activation(
                hT[:, b, :, 0:n], PS[:, trb, 0:256].rearrange("p (f n) -> p f n", f=2)[:, :, 0:n], ACT.Copy))

        t_WI = {}
        t_hnew = {b: t_h[b] for b in range(NB)}
        t_wt_free = None
        lastg = None
        for l in range(5):
            cur, nxt = l % 2, (l + 1) % 2
            w = [t_wt_free] if t_wt_free else []
            twt = load(S, wt[:, :, :], a["weightT"][l].rearrange("(k p) n -> p k n", p=128), s_wt, *w)
            for _ in range(NPAN if l == 0 else 0):
                issue_panel()
            evs = []
            for m in range(2):
                bank = 2 + m
                for (lo, hi, bk) in ((0, 512, 2 + m), (512, 768, 4 + m)):
                    T.w(twt, tw, *([t_rz_free[m], t_nn_free[m]] if m in t_rz_free else []))
                    for k in range(2):
                        ins = T.e.matmul(PS[:, bk, 0:hi - lo], lhsT=wt[:, k, m * 128:(m + 1) * 128], rhs=wih[:, k, lo:hi],
                                         start=(k == 0), stop=(k == 1))
                    tt = T.did(ins)
                    free = [lastg] if lastg else []
                    ev = A.did(A.w(tt, *free).activation(WI[l % 2][:, m, lo:hi], PS[:, bk, 0:hi - lo], ACT.Copy))
                    evs.append(ev)
                t_rz_free[m] = evs[-2]
                t_nn_free[m] = evs[-1]
            t_wt_free = tt
            t_WI[l] = evs[-1]
            agg_done = {}
            queue = []
            pendT = []
            for q in range(NG + 1):
                if q < NG:
                    m = cols_of(q)
                    for k in range(5):
                        i = (l * NG + q) * 5 + k
                        T.w(t_panel[i], *([t_agg_free[0]] if 0 in t_agg_free and k == 0 else []))
                        for s5 in range(5):
                            sb = 5 * k + s5
                            T.w(t_hnew[sb])
                            for f in range(2):
                                ins = T.e.matmul(PS[:, f, 0:m], lhsT=hbuf[cur][:, sb, f * 128:(f + 1) * 128],
                                                 rhs=pan[i % NPAN][:, s5, 0:m], start=(sb == 0), stop=(sb == NB - 1))
                        t_pan_free[i] = T.did(ins)
                        issue_panel()
                    t_mm = t_pan_free[i]
                    ag = aggT[q % 2]
                    w = [t_agg_ev[q % 2]] if t_agg_ev[q % 2] else []
                    e0 = A.did(A.w(t_mm, *w).activation(ag[:, 0, 0:m], PS[:, 0, 0:m], ACT.Copy))
                    e1 = V.did(V.w(t_mm, *w).tensor_copy(ag[:, 1, 0:m], PS[:, 1, 0:m]))
                    agg_done[q] = (e0, e1)
                    t_agg_free[0] = e0
                    T_agg_extra = e1
                if q >= 1:
                    p = q - 1
                    e0, e1 = agg_done[p]
                    T.w(e1)
                    for b in range(4 * p, min(4 * p + 4, NB)):
                        tk, t_nn, n, trb = gru(l, b, aggT[p % 2], e0, cur, nxt)
                        t_hnew[b] = tk
                        lastg = t_nn
                        pendT.append((b, n, trb, nxt, tk, t_nn))
                        if len(pendT) > 1:
                            retranspose(*pendT.pop(0))
                    t_agg_ev[p % 2] = t_nn
                if q < NG:
                    T.w(agg_done[q][1])
            while pendT:
                retranspose(*pendT.pop(0))
        meet()
        top[0] = base_top
        X = mk(NB, D)
        hold = hbuf[1]
        t0 = G.did(G.e.memset(X[:, 24, :], 0.0))
        tx = load_rows(X, a["x"], S, s_x, t0)
        for b in range(NB):
            tX = V.did(V.w(tx).tensor_tensor(X[:, b, :], X[:, b, :], hold[:, b, :], ALU.add))
        meet()
        x_top = top[0]

        def transpose_rows(Y, b, dstT, bank, *ticks):
            T.w(*ticks)
            for f in range(2):
                ins = T.e.transpose(PS[:, bank, f * 128:(f + 1) * 128], Y[:, b, f * 128:(f + 1) * 128], ident)
            tt = T.did(ins)
            return A.did(A.w(tt).activation(dstT, PS[:, bank, 0:256].rearrange("p (f n) -> p f n", f=2), ACT.Copy))

        Y = mk(NB, D)
        W1 = mk(2, 1024)
        b1c = mk(8)
        Wg = mk(8, 8)
        Wd = mk(8 * 2048)
        bg = mk(8)
        bd = mk(256)
        yT = [mk(2, 512) for _ in range(2)]
        gt = mk(NB, 8)
        lgt = mk(NB, 8)
        OH = mk(NB, 8)
        sc = mk(NB, 8)
        rst = mk(NB, 8)
        mm = mk(2, NB)
        gT = mk(128)
        s_w = new_sem()
        load(S, W1[:, :, :], a["W1"].rearrange("(k p) n -> p k n", p=128), s_w)
        load(S, b1c, a["b1T"], s_w)
        load(S, Wg[:, :, :], a["Wg"].rearrange("(k p) n -> p k n", p=128), s_w)
        load(S, bg, a["bg"].unsqueeze(0).partition_broadcast(128), s_w)
        tw = load(S, bd[0:8], a["bd"], s_w)
        s_wd = new_sem()
        for e in range(8):
            t_wd = load(S, Wd[:, e * 2048:(e + 1) * 2048].rearrange("p (k n) -> p k n", k=8),
                        a["Wd"][e].rearrange("(k p) n -> p k n", p=128), s_wd)
        t_y = layernorm(Y, X, [tX])
        ff_top = top[0]
        HTs = [mk(8, 512) for _ in range(2)]
        NH = 3
        gl = mk(512)
        hrow = [mk(1024) for _ in range(NH)]
        s_hr = [new_sem() for _ in range(NH)]
        free = {i: None for i in range(8)}

        def fw(*banks):
            return [free[b] for b in banks if free[b]]

        t_hr, t_htfree = {}, {}
        for q in range(NG):
            nbk = min(4, NB - 4 * q)
            m = nbk * 128
            HT = HTs[q % 2]
            for j in range(nbk):
                bank = 6 + j % 2
                b = 4 * q + j
                free[bank] = transpose_rows(Y, b, yT[q % 2][:, :, j * 128:(j + 1) * 128], bank, t_y[b], *fw(bank))
            for c in range(8):
                bank = c % 2
                T.w(tw, *fw(bank, 6, 7))
                for k in range(2):
                    ins = T.e.matmul(PS[:, bank, 0:m], lhsT=W1[:, k, c * 128:(c + 1) * 128], rhs=yT[q % 2][:, k, 0:m],
                                     start=(k == 0), stop=(k == 1))
                tt = T.did(ins)
                free[bank] = t_ht = A.did(A.w(tt, *([t_htfree[q - 2]] if q >= 2 else [])).activation(
                    HT[:, c, 0:m], PS[:, bank, 0:m], ACT.Gelu, bias=b1c[:, c:c + 1]))
            T.w(t_ht, *fw(6))
            for k in range(8):
                ins = T.e.matmul(PS[0:8, 6, 0:m], lhsT=Wg[:, k, :], rhs=HT[:, k, 0:m], start=(k == 0), stop=(k == 7))
            tt = T.did(ins)
            free[6] = t_gl = A.did(A.w(tt, *([t_glf] if q else [])).activation(gl[0:8, 0:m], PS[0:8, 6, 0:m], ACT.Copy))
            for j in range(nbk):
                b = 4 * q + j
                cs = slice(j * 128, (j + 1) * 128)
                r = b % 2
                for h in range(2):
                    bank = 2 + 2 * r + h
                    T.w(*fw(bank))
                    for k in range(4):
                        ins = T.e.transpose(PS[:, bank, k * 128:(k + 1) * 128], HT[:, 4 * h + k, cs], ident)
                    t_htfree[q] = tt = T.did(ins)
                    w = [t_hr[b - NH]] if b >= NH else []
                    o = hrow[b % NH][:, h * 512:(h + 1) * 512]
                    if h == 0:
                        free[bank] = A.did(A.w(tt, *w).activation(o, PS[:, bank, :], ACT.Copy))
                    else:
                        free[bank] = V.did(V.w(tt, *w).tensor_copy(o, PS[:, bank, :]))
                t_hr[b] = load(S, HR[b * 128:(b + 1) * 128, :], hrow[b % NH], s_hr[b % NH], *fw(2 + 2 * r, 3 + 2 * r))
            T.w(t_gl, *fw(7))
            for j in range(nbk):
                ins = T.e.transpose(PS[:, 7, j * 8:(j + 1) * 8], gl[0:8, j * 128:(j + 1) * 128], ident[0:8, 0:8])
            tt = t_glf = T.did(ins)
            free[7] = t_lg = V.did(V.w(tt).tensor_tensor(
                lgt[:, 4 * q:4 * q + nbk, :], PS[:, 7, 0:nbk * 8].rearrange("p (j e) -> p j e", e=8),
                bc(bg.unsqueeze(1), [128, nbk, 8]), ALU.add))
        pmx, psm = mm[:, 0, :], mm[:, 1, :]

        def over(v):
            return bc(v.unsqueeze(2), [128, NB, 8])

        tk = V.did(V.w(t_lg).tensor_reduce(pmx, lgt, AX, ALU.max))
        tk = V.did(V.w(tk).tensor_tensor(lgt, lgt, over(pmx), ALU.subtract))
        tk = A.did(A.w(tk).activation(lgt, lgt, ACT.Exp))
        tk = V.did(V.w(tk).tensor_reduce(psm, lgt, AX, ALU.add))
        tk = V.did(V.w(tk).reciprocal(psm, psm))
        tk = V.did(V.w(tk).tensor_tensor(lgt, lgt, over(psm), ALU.mult))
        tk = V.did(V.w(tk).tensor_reduce(pmx, lgt, AX, ALU.max))
        t0 = V.did(V.e.memset(rst, 1.0))
        t0 = V.did(V.w(t0).memset(rst[:, :, 0:1], 0.0))
        tk = V.did(V.w(tk).tensor_tensor(OH, lgt, over(pmx), ALU.is_equal))
        tk = V.did(V.w(tk, t0).tensor_tensor_scan(sc.rearrange("p b e -> p (b e)"), rst.rearrange("p b e -> p (b e)"),
                                                  OH.rearrange("p b e -> p (b e)"), 0.0, ALU.mult, ALU.add))
        tk = V.did(V.w(tk).scalar_tensor_tensor(OH, sc, 1.0, OH, ALU.is_equal, ALU.mult))
        t_gt = V.did(V.w(tk).tensor_tensor(gt, OH, over(pmx), ALU.mult))
        tk = V.did(V.w(t_gt).tensor_scalar(OH[:, 24, :], OH[:, 24, :], tailc, None, ALU.mult))
        meet(*[t_hr[NB - 1 - i] for i in range(NH)])
        top[0] = ff_top
        pos, posi, t_pos, eid, t_eid = route(OH, NB, 8, NT0, tk)
        tk = V.did(V.w(t_eid).tensor_scalar(eid, eid, 8.0, None, ALU.mult))
        eo = mk(NT0, dt=I32)
        t_eo = V.did(V.w(tk).tensor_copy(eo, eid))
        ia, ib = mk(NB, dt=I32), mk(NB, dt=I32)
        fa = mk(NB)
        tok = mk(NT0, dt=I32)
        tk = V.did(V.w(t_pos).tensor_single_scalar(ia, posi, 127, ALU.bitwise_and))
        t2 = V.did(V.e.tensor_single_scalar(ib, posi, 7, ALU.logical_shift_right))
        tk = V.did(V.w(tk).tensor_copy(fa, ia))
        t2 = V.did(V.w(t2).tensor_copy(pos, ib))
        tk = V.did(V.w(tk, t2).scalar_tensor_tensor(fa, fa, float(NT0), pos, ALU.mult, ALU.add))
        tk = V.did(V.w(tk).tensor_copy(ia, fa))
        s_ti = new_sem()
        G.w(tk)
        for b in range(NB):
            n = rows_of(b)
            ti = s_ti.add(G.e.indirect_dma_start(TI[:, :], bass.IndirectOffsetOnAxis(ap=ia[0:n, b:b + 1], axis=0),
                                                 tokid[0:n, b:b + 1], None), 16)
        ti = load(S, tok, TI.rearrange("(p t) o -> p (t o)", p=128), new_sem(), ti)
        NRG = 3
        hs = [mk(1024) for _ in range(NRG)]
        hsT = [mk(8, 128) for _ in range(2)]
        og = [mk(256) for _ in range(2)]
        s_hs = [new_sem() for _ in range(NRG)]
        s_og = [new_sem(), new_sem()]
        eregs = [nc.tensor.alloc_register(f"ex{i}") for i in range(8)]
        t_g, t_tr_, t_cp, t_mm, t_ev, t_st = ({} for _ in range(6))
        for i in range(NT0 + 1):
            if i < NT0:
                G.w(ti, *([t_tr_[i - NRG]] if i >= NRG else []))
                t_g[i] = s_hs[i % NRG].add(G.e.indirect_dma_start(
                    hs[i % NRG], None, HR[:, :], bass.IndirectOffsetOnAxis(ap=tok[:, i:i + 1], axis=0)), 16)
                T.w(t_g[i])
                r = i % 2
                cps = []
                for h in range(2):
                    bank = 2 * r + h
                    T.w(*([t_cp[i - 2][h]] if i >= 2 else []))
                    for k in range(4):
                        ins = T.e.transpose(PS[:, bank, k * 128:(k + 1) * 128],
                                            hs[i % NRG][:, (4 * h + k) * 128:(4 * h + k + 1) * 128], ident)
                    tt = T.did(ins)
                    o = hsT[r][:, 4 * h:4 * h + 4, :].rearrange("p k n -> p (k n)")
                    w = [t_mm[i - 2]] if i >= 2 else []
                    cps.append(A.did(A.w(tt, *w).activation(o, PS[:, bank, :], ACT.Copy)) if h == 0 else
                               V.did(V.w(tt, *w).tensor_copy(o, PS[:, bank, :])))
                t_tr_[i], t_cp[i] = tt, cps
            if i >= 1:
                j = i - 1
                r = j % 2
                T.w(*t_cp[j], t_wd, t_eo, *([t_ev[j - 2]] if j >= 2 else []))
                if j % 8 == 0:
                    T.e.reg_load(eregs, eo[0:1, j:j + 8])
                v = T.e.snap(eregs[j % 8], min_val=0, max_val=7 * 8)
                for k in range(8):
                    ins = T.e.matmul(PS[:, 4 + r, 0:256], lhsT=hsT[r][:, k, :], rhs=Wd[:, bass.ds(v * 256 + k * 256, 256)],
                                     start=(k == 0), stop=(k == 7))
                t_mm[j] = T.did(ins)
                t_ev[j] = V.did(V.w(t_mm[j], *([t_st[j - 2]] if j >= 2 else [])).tensor_copy(og[r], PS[:, 4 + r, 0:256]))
                t_st[j] = load(S, YS0[j * 128:(j + 1) * 128, :], og[r], s_og[r], t_ev[j])
        NRG = 4
        yg = [mk(256) for _ in range(NRG)]
        s_yg = [new_sem() for _ in range(NRG)]
        t_a1 = {}
        t_z = G.did(G.e.memset(yg[(NB - 1) % NRG], 0.0))
        for b in range(NB):
            n = rows_of(b)
            r = b % 2
            tt = T.did(T.w(t_gt, *fw(6)).transpose(PS[0:8, 6, 0:128], gt[:, b, :], ident))
            tk = free[6] = A.did(A.w(tt, *fw(7)).activation(gT[0:8], PS[0:8, 6, 0:128], ACT.Copy))
            tt = T.did(T.w(tk, *fw(7)).matmul(PS[:, 7, 0:256], lhsT=gT[0:8], rhs=bd[0:8], start=True, stop=True))
            free[7] = tX = V.did(V.w(tt).tensor_tensor(X[:, b, :], X[:, b, :], PS[:, 7, 0:256], ALU.add))
            G.w(t_pos, t_st[NT0 - 1], t_st[NT0 - 2], t_z, *([t_a1[b - NRG]] if b >= NRG else []))
            tg_ = s_yg[b % NRG].add(G.e.indirect_dma_start(
                yg[b % NRG][0:n], None, YS0[:, :], bass.IndirectOffsetOnAxis(ap=posi[0:n, b:b + 1], axis=0)), 16)
            t_a1[b] = tX = V.did(V.w(tg_, tX).scalar_tensor_tensor(
                X[0:n, b, :], yg[b % NRG][0:n], pmx[0:n, b:b + 1], X[0:n, b, :], ALU.mult, ALU.add))
        meet()
        top[0] = x_top

        lin = mk(52, 16, 8)

        def tiles(x, t, n):
            return x[:, t % 52:t % 52 + n, t // 52, :]

        sl = mk(T2)
        nsl = mk(T2)
        slb = mk(T2, dt=BF)
        idxD = mk(T2, dt=I32)
        fin_top = top[0]
        HB = mk(NB, 272)
        gat_top = top[0]
        Y = mk(NB, D)
        Wa = mk(2, 272)
        av5 = mk(5, 256)
        yT = [mk(2, 128) for _ in range(2)]
        u1 = [mk(256) for _ in range(2)]
        u2 = mk(2, 256)
        hq = mk(8)
        s_w = new_sem()
        load(S, Wa[:, :, 0:256], a["Wgat"].rearrange("(k p) n -> p k n", p=128), s_w)
        tw = load(S, av5.rearrange("p a b -> p (a b)"), a["a5"].rearrange("a b -> (a b)").unsqueeze(0).partition_broadcast(128), s_w)
        t_y = layernorm(Y, X, [tX])
        cS, cD, a5h = av5[:, 0, :], av5[:, 1, :], av5[:, 4, :]
        t0 = V.did(V.w(tw).tensor_tensor(cS, cS, av5[:, 2, :], ALU.subtract))
        t1 = V.did(V.e.tensor_tensor(cD, cD, av5[:, 2, :], ALU.add))
        t_c = V.did(V.e.tensor_scalar(a5h, a5h, 0.5, None, ALU.mult))
        for i, (c, tk) in enumerate(((cS, t0), (cD, t1))):
            tk = V.did(V.w(tk, t_c).tensor_tensor(u2, Wa[:, :, 0:256], bc(c.unsqueeze(1), [128, 2, 256]), ALU.mult))
            t_c = V.did(V.w(tk).tensor_reduce(Wa[:, :, 256 + 8 * i:264 + 8 * i],
                                              u2.rearrange("p k (h d) -> p k h d", h=8), AX, ALU.add))
        fa = mk(T2)
        tk = V.did(V.e.tensor_copy(fa, srcc))
        bl2 = bc(blkf.unsqueeze(2), [128, T2 // 2, 2])
        tk = t_sl = V.did(V.w(tk).scalar_tensor_tensor(sl.rearrange("p (a b) -> p a b", b=2), bl2, -128.0,
                                                       fa.rearrange("p (a b) -> p a b", b=2), ALU.mult, ALU.add))
        V.did(V.w(tk).tensor_copy(slb, sl))
        V.did(V.e.tensor_scalar(nsl, sl, -1.0, None, ALU.mult))
        tk = V.did(V.e.tensor_copy(fa, dstc))
        tk = V.did(V.w(tk).tensor_scalar(fa, fa, float(N - 1), None, ALU.min))
        t_ix = V.did(V.w(tk).tensor_copy(idxD, fa))
        tk = V.did(V.w(t_sl).tensor_scalar(blkf, blkf, 8.0, None, ALU.mult))
        t_blko = V.did(V.w(tk).tensor_copy(blko, blkf))
        s_row = new_sem()
        ev, mmt, ev2, t_n2 = {}, {}, {}, {}

        def turn(b):
            r = b % 2
            ev[b] = transpose_rows(Y, b, yT[r], 6 + r, t_y[b], *([ev[b - 2], mmt[b - 2]] if b >= 2 else []))

        turn(0)
        for b in range(NB):
            if b + 1 < NB:
                turn(b + 1)
            r = b % 2
            hr = HB[:, b, :]
            T.w(ev[b], tw, t_c, *([ev2[b - 2], t_n2[b - 2]] if b >= 2 else []))
            for k in range(2):
                ins = T.e.matmul(PS[:, r, 0:272], lhsT=yT[r][:, k, :], rhs=Wa[:, k, :], start=(k == 0), stop=(k == 1))
            mmt[b] = T.did(ins)
            ev2[b] = A.did(A.w(mmt[b]).activation(
                hr[:, 0:256], PS[:, r, 0:256], ACT.Copy))
            tk = V.did(V.w(ev2[b]).tensor_tensor(u1[r], hr[:, 0:256], a5h, ALU.mult))
            tk = V.did(V.w(tk).tensor_tensor(u1[r], u1[r], hr[:, 0:256], ALU.mult))
            tk = V.did(V.w(tk, *([t_n2[b - 1]] if b else [])).tensor_reduce(
                hq, u1[r].rearrange("p (h d) -> p h d", h=8), AX, ALU.add))
            t_n2[b] = V.did(V.w(tk).tensor_tensor(hr[:, 256:272].rearrange("p (i h) -> p i h", i=2),
                                                  PS[:, r, 256:272].rearrange("p (i h) -> p i h", i=2),
                                                  bc(hq.unsqueeze(1), [128, 2, 8]), ALU.add))
            t_hd = load(S, HD[b * 128:(b + 1) * 128, :], hr, s_row, t_n2[b], ev2[b])
        meet(t_hd)
        top[0] = gat_top
        NR = 8
        Dg = [mk(4, 272) for _ in range(NR)]
        df = [mk(2, 256) for _ in range(2)]
        ab = [mk(4, 128) for _ in range(2)]
        sq = [mk(4, 128) for _ in range(2)]
        OT = [mk(2, 128) for _ in range(2)]
        msk = mk(2, 8)
        a45 = mk(4)
        s_w = new_sem()
        load(S, a45[:, 0:2], a["a4c"], s_w)
        load(S, a45[:, 2:4], a["a5c"], s_w)
        tw = load(S, msk[:, :, :], a["c_mask"], s_w)
        V.w(tw)
        t_a = V.did(V.e.tensor_scalar(a45[:, 2:4], a45[:, 2:4], -0.5, None, ALU.mult))
        s_g = [new_sem() for _ in range(NR)]
        s_sp = [new_sem() for _ in range(NR)]
        t_df, t_tr, t_sq, t_ab, t_mm, t_lin, t_bc, t_ot, t_hs, t_l1, t_sp = ({} for _ in range(11))
        NQ = T2 // 4
        pregs = [nc.tensor.alloc_register(f"row{i}") for i in range(8)]
        hbf = HB.rearrange("p b n -> p (b n)")

        def expand(p):
            r = p % 2
            T.w(*([t_ot[p - 1]] if p else []))
            for j in range(2):
                ins = T.e.matmul(PS[:, 0, j * 128:(j + 1) * 128],
                                 lhsT=bc(slb[:, 2 * p + j:2 * p + j + 1], [128, 128]), rhs=identb, start=True, stop=True)
            t_bc[p] = T.did(ins)
            t_ot[p] = V.did(V.w(t_bc[p], *([t_hs[p - 2]] if p >= 2 else [])).tensor_scalar(
                OT[r], PS[:, 0, 0:256].rearrange("p (j n) -> p j n", j=2), pidx, None, ALU.is_equal))

        def sources(p):
            r, i = p % 2, p // 2
            n, j0 = i % NR, 2 * (p % 2)
            T.w(t_ot[p], t_blko, *([t_l1[p - 2], t_df[p - 2]] if p >= 2 else []))
            if p % 8 == 0:
                T.e.reg_load(pregs, blko[0:1, p:p + 8])
            v = T.e.snap(pregs[p % 8], min_val=0, max_val=24 * 8)
            rhs = hbf[:, bass.ds(v * 34, 264)]
            for j in range(2):
                ins = T.e.matmul(PS[:, 1 + 2 * r + j, 0:264], lhsT=OT[r][:, j, :], rhs=rhs, start=True, stop=True)
            t_hs[p] = T.did(ins)
            pv = PS[:, 1 + 2 * r:3 + 2 * r, :]
            t_df[p] = V.did(V.w(t_hs[p], t_g[i], *([t_tr[p - 2]] if p >= 2 else [])).tensor_tensor(
                df[r], Dg[n][:, j0:j0 + 2, 0:256], pv[:, :, 0:256], ALU.subtract))
            t_l1[p] = V.did(V.e.tensor_tensor(tiles(lin, 2 * p, 2), pv[:, :, 256:264], Dg[n][:, j0:j0 + 2, 264:272],
                                              ALU.add))

        def columns(p):
            r = p % 2
            T.w(t_df[p], *([t_ab[p - 2]] if p >= 2 else []))
            for k in range(4):
                ins = T.e.transpose(PS[:, 5 + r, k * 128:(k + 1) * 128],
                                    df[r][:, k // 2, (k % 2) * 128:(k % 2 + 1) * 128], ident)
            t_tr[p] = T.did(ins)
            A.w(t_tr[p], *([t_mm[p - 2]] if p >= 2 else []))
            t_ab[p] = A.did(A.e.activation(ab[r].rearrange("p k n -> p (k n)"), PS[:, 5 + r, :], ACT.Abs))
            for f in range(2):
                tk = A.did(A.w(t_ab[p], t_a).activation(sq[r][:, f::2, :], ab[r][:, f::2, :], ACT.Identity,
                                                        bias=a45[:, f:f + 1], scale=a45[:, 2 + f:3 + f]))
            t_q[p] = tk

        def products(p):
            r = p % 2
            t_sq[p] = V.did(V.w(t_q[p]).tensor_tensor(sq[r], sq[r], ab[r], ALU.mult))

        def weigh(p):
            r = p % 2
            T.w(t_sq[p], tw, *([t_lin[p - 1]] if p else []))
            for j in range(2):
                for f in range(2):
                    ins = T.e.matmul(PS[:, 7, j * 8:(j + 1) * 8], lhsT=sq[r][:, 2 * j + f, :],
                                     rhs=msk[:, f, :], start=(f == 0), stop=(f == 1))
            t_mm[p] = T.did(ins)
            ln = tiles(lin, 2 * p, 2)
            t_lin[p] = V.did(V.w(t_mm[p], t_l1[p]).tensor_tensor(
                ln, ln, PS[:, 7, 0:16].rearrange("p (j h) -> p j h", h=8), ALU.add))

        t_g, t_q = {}, {}
        NP2 = T2 // 2
        expand(0)
        for p in range(NP2 + 2):
            if p < NP2 and p % 2 == 0:
                i = p // 2
                n = i % NR
                G.w(t_ix, *([t_l1[p - 2 * NR + 1], t_df[p - 2 * NR + 1], t_sp[i - NR]] if i >= NR else []))
                for j in range(4):
                    t = 4 * i + j
                    t_g[i] = s_g[n].add(G.e.indirect_dma_start(
                        Dg[n][:, j, :], None, HD[:, :], bass.IndirectOffsetOnAxis(ap=idxD[:, t:t + 1], axis=0)), 16)
                t_sp[i] = load(S, SPL[i].rearrange("p (j d) -> p j d", j=4), Dg[n][:, :, 0:256], s_sp[n], t_g[i])
            if 1 <= p <= NP2:
                columns(p - 1)
            if p + 1 < NP2:
                expand(p + 1)
            if p < NP2:
                sources(p)
            if 1 <= p <= NP2:
                products(p - 1)
            if p >= 2:
                weigh(p - 2)
        t_spill = [t_sp[i] for i in range(NQ - NR, NQ)]
        meet(*t_spill)
        top[0] = fin_top
        L = 52 * 128
        AT = mk(L)
        PEN = mk(L + 1)
        SR = mk(L)
        srb = mk(52, 16, 8)
        sm4 = mk(4)
        q8 = mk(16, 4)
        lk = mk(4, 16)
        cc = mk(1)
        al = lin
        t_al = V.did(V.e.scalar_tensor_tensor(al, lin, 0.2, lin, ALU.mult, ALU.max))
        t_sb = V.did(V.e.tensor_copy(srb, bc(srcc.rearrange("p (a g) -> p g a", g=52).unsqueeze(3), [128, 52, 16, 8])))
        alv = al.rearrange("p g a h -> p g (a h)")
        srv = srb.rearrange("p g a h -> p g (a h)")
        ev = {}
        for k in range(13):
            for n, (v, dst, eng) in enumerate(((alv, AT, A), (srv, SR, V))):
                bank = 2 * (k % 2) + n
                T.w(t_al, t_sb, *([ev[(k - 2, n)]] if k >= 2 else []))
                for j in range(4):
                    ins = T.e.transpose(PS[:, bank, j * 128:(j + 1) * 128], v[:, 4 * k + j, :], ident)
                tt = T.did(ins)
                o = dst[:, 512 * k:512 * (k + 1)]
                if n == 0:
                    ev[(k, n)] = A.did(A.w(tt).activation(o, PS[:, bank, :], ACT.Copy))
                else:
                    ev[(k, n)] = V.did(V.w(tt).tensor_copy(o, PS[:, bank, :]))
        t_at, t_sr = ev[(12, 0)], ev[(12, 1)]
        V.did(V.w(t_sr).memset(PEN[:, 0:1], -BIG))
        V.did(V.e.memset(PEN[:, L:L + 1], -BIG))
        tk = V.did(V.e.tensor_tensor(PEN[:, 1:L], SR[:, 1:L], SR[:, 0:L - 1], ALU.not_equal))
        t_pen = V.did(V.w(tk).tensor_scalar(PEN[:, 1:L], PEN[:, 1:L], -BIG, None, ALU.mult))
        V.did(V.w(t_pen).tensor_reduce(sm4[:, 1:2], PEN[:, 1:L], AX, ALU.min))
        V.did(V.e.tensor_copy(sm4[:, 2:3], SR[:, 0:1]))
        V.did(V.e.tensor_copy(sm4[:, 3:4], SR[:, L - 1:L]))
        tk = V.did(V.w(t_pen, t_at).tensor_tensor_scan(AT, PEN[:, 0:L], AT, -BIG, ALU.add, ALU.max))
        tk = V.did(V.w(tk).tensor_copy(sm4[:, 0:1], AT[:, L - 1:L]))
        s_q = [new_sem() for _ in range(6)]
        tk = load(S, Q1[:, :], sm4, s_q[0], tk)
        tk = load(S, q8[0:8, :, :], Q1.rearrange("(a h) f -> h a f", h=8), s_q[1], tk)
        link, ch = lk[0:8, 0, :], lk[0:8, 1, :]
        xs, cr = lk[0:8, 2, :], lk[0:8, 3, :]
        V.did(V.w(tk).memset(link[:, 0:1], -BIG))
        tk = V.did(V.e.tensor_tensor(link[:, 1:16], q8[0:8, 1:16, 2], q8[0:8, 0:15, 3], ALU.not_equal))
        tk = V.did(V.w(tk).tensor_scalar(link[:, 1:16], link[:, 1:16], -BIG, None, ALU.mult))
        tk = V.did(V.w(tk).tensor_tensor(ch, link, q8[0:8, :, 1], ALU.min))
        tk = V.did(V.w(tk).tensor_tensor_scan(xs, ch, q8[0:8, :, 0], -BIG, ALU.add, ALU.max))
        V.did(V.e.memset(cr[:, 0:1], -BIG))
        tk = V.did(V.w(tk).tensor_tensor(cr[:, 1:16], xs[:, 0:15], link[:, 1:16], ALU.add))
        tk = load(S, Q2.rearrange("(a h) f -> h (a f)", h=8), cr, s_q[2], tk, allow_slow_non_contiguous=True)
        tk = load(S, cc, Q2[:, :], s_q[3], tk)
        tk = V.did(V.w(tk).tensor_tensor(AT[:, 0:1], AT[:, 0:1], cc, ALU.max))
        tk = V.did(V.w(tk).tensor_tensor_scan(AT, PEN[:, 0:L], AT, -BIG, ALU.add, ALU.max))
        rA, rP = AT[:, ::-1], PEN[:, 1:L + 1][:, ::-1]
        tk = V.did(V.w(tk).tensor_tensor_scan(rA, rP, rA, -BIG, ALU.add, ALU.max))
        tk = load(S, Q3[:, :], AT[:, 0:1], s_q[4], tk)
        tk = load(S, q8[0:8, :, 0:1], Q3.rearrange("(a h) f -> h a f", h=8), s_q[5], tk, allow_slow_non_contiguous=True)
        V.did(V.w(tk).memset(ch[:, 15:16], -BIG))
        tk = V.did(V.e.tensor_tensor(ch[:, 0:15], link[:, 1:16], q8[0:8, 0:15, 1], ALU.min))
        tk = V.did(V.w(tk).tensor_tensor_scan(xs[:, ::-1], ch[:, ::-1], q8[0:8, :, 0][:, ::-1], -BIG, ALU.add, ALU.max))
        V.did(V.e.memset(cr[:, 15:16], -BIG))
        tk = V.did(V.w(tk).tensor_tensor(cr[:, 0:15], xs[:, 1:16], link[:, 1:16], ALU.add))
        s_q2 = [new_sem(), new_sem()]
        tk = load(S, Q4.rearrange("(a h) f -> h (a f)", h=8), cr, s_q2[0], tk, allow_slow_non_contiguous=True)
        tk = load(S, cc, Q4[:, :], s_q2[1], tk)
        tk = V.did(V.w(tk).tensor_tensor(AT[:, L - 1:L], AT[:, L - 1:L], cc, ALU.max))
        t_mx = V.did(V.w(tk).tensor_tensor_scan(rA, rP, rA, -BIG, ALU.add, ALU.max))
        ev = {}
        for k in range(13):
            bank = k % 4
            T.w(t_mx, *([ev[k - 4]] if k >= 4 else []))
            for j in range(4):
                g = 4 * k + j
                ins = T.e.transpose(PS[:, bank, j * 128:(j + 1) * 128], AT[:, g * 128:(g + 1) * 128], ident)
            tt = T.did(ins)
            o = alv[:, 4 * k:4 * k + 4, :]
            ev[k] = V.did(V.w(tt).tensor_tensor(o, o, PS[:, bank, :].rearrange("p (g m) -> p g m", g=4), ALU.subtract))
        lv = lin.rearrange("p g a h -> p (g a h)")
        t_e = A.did(A.w(ev[12]).activation(lv, lv, ACT.Exp))
        meet()
        top[0] = fin_top
        acc = mk(NB, 264)
        NR = 4
        Dg = [mk(4, 256) for _ in range(NR)]
        Wv = [mk(2, 264) for _ in range(3)]
        On = [mk(2, 128) for _ in range(3)]
        Ab = [mk(2, 128) for _ in range(2)]
        s_g = [new_sem() for _ in range(NR)]
        regs = [nc.vector.alloc_register(f"blk{i}") for i in range(8)]
        accf = acc.rearrange("p b n -> p (b n)")
        t_acc = V.did(V.e.memset(accf, 0.0))
        t_wv, t_wg, t_on, t_mm, t_ce, t_ac, t_g = ({} for _ in range(7))
        for i in range(NPAIR + 1):
            if i < NPAIR:
                q, r = i // 2, i % 3
                n = q % NR
                if i % 2 == 0:
                    t_g[q] = load(S, Dg[n], SPL[q].rearrange("p (j d) -> p j d", j=4), s_g[n],
                                  *([t_wv[2 * (q - NR) + 1], t_wg[2 * (q - NR) + 1], t_wv[2 * (q - NR)], t_wg[2 * (q - NR)]]
                                    if q >= NR else []))
                free3 = [t_mm[i - 3]] if i >= 3 else []
                ee = tiles(lin, 2 * i, 2)
                t_ce[i] = A.did(A.w(t_e, *free3).activation(Wv[r][:, :, 256:264], ee, ACT.Copy))
                for j in range(2):
                    tk = A.did(A.w(*([t_on[i - 2]] if i >= 2 else [])).activation(
                        Ab[i % 2][:, j, :], iota, ACT.Abs, bias=nsl[:, 2 * i + j:2 * i + j + 1]))
                t_on[i] = A.did(A.w(tk).activation(On[r], Ab[i % 2], ACT.Relu, bias=ones[:, 0:1], scale=-1.0))
                k0 = 2 * (i % 2)
                outs = []
                for j, g in ((0, V), (1, G)):
                    outs.append(g.did(g.w(t_e, t_g[q], *free3).tensor_tensor(
                        Wv[r][:, j, 0:256].rearrange("p (h d) -> p h d", h=8),
                        Dg[n][:, k0 + j, :].rearrange("p (h d) -> p h d", h=8),
                        bc(ee[:, j, :].unsqueeze(2), [128, 8, 32]), ALU.mult)))
                t_wv[i], t_wg[i] = outs
                T.w(t_wv[i], t_wg[i], t_on[i], t_ce[i], *([t_ac[i - 3]] if i >= 3 else []))
                for j in range(2):
                    ins = T.e.matmul(PS[:, r, 0:264], lhsT=On[r][:, j, :], rhs=Wv[r][:, j, :], start=(j == 0), stop=(j == 1))
                t_mm[i] = T.did(ins)
            if i >= 1:
                p = i - 1
                if p % 8 == 0:
                    V.e.reg_load(regs[0:min(8, NPAIR - p)], blko[0:1, p:p + min(8, NPAIR - p)])
                v = V.e.snap(regs[p % 8], min_val=0, max_val=24 * 8)
                dst = accf[:, bass.ds(v * 33, 264)]
                t_acc = t_ac[p] = V.did(V.w(t_acc, t_mm[p]).tensor_tensor(dst, dst, PS[:, p % 3, 0:264], ALU.add))
        sd = acc[:, :, 256:264]
        tk = V.did(V.w(t_acc).tensor_scalar(sd, sd, 1.0e-16, None, ALU.add))
        tk = V.did(V.w(tk).reciprocal(sd, sd))
        o4 = acc[:, :, 0:256].rearrange("p b (h d) -> p b h d", h=8)
        for b in range(NB):
            g = (V, G)[b % 2]
            t1 = g.did(g.w(tk).tensor_tensor(o4[:, b], o4[:, b], bc(sd[:, b].unsqueeze(2), [128, 8, 32]), ALU.mult))
            tX = V.did(V.w(t1).tensor_tensor(X[:, b, :], X[:, b, :], acc[:, b, 0:256], ALU.add))
        meet()
        top[0] = x_top

        Y = mk(NB, D)
        W1 = mk(16 * 1024)
        W2 = mk(16 * 1024)
        hT = [mk(4, 128) for _ in range(3)]
        s_xd = new_sem()
        t_xd = load(S, XD[:, :], X.rearrange("p b d -> p (b d)"), s_xd, tX)
        top[0] = rec_top
        gw = mk(2, 16)
        gbb = mk(16)
        b1c = mk(16 * 4)
        b2 = mk(256)
        gT = [mk(128) for _ in range(2)]
        gt = mk(NB, 16)
        lgt = mk(NB, 16)
        s2 = mk(NB, 16)
        rst = mk(NB, 16)
        mm = mk(4, NB)
        s_w = new_sem()
        load(S, gw[:, :, :], a["gate_w"].rearrange("(k p) n -> p k n", p=128), s_w)
        load(S, gbb, a["gate_b"].unsqueeze(0).partition_broadcast(128), s_w)
        load(S, b1c, a["b1m"].rearrange("p e c -> p (e c)"), s_w)
        tw = load(S, b2[0:16], a["b2"], s_w)
        s_e = new_sem()
        for e in range(16):
            load(S, W1[:, e * 1024:(e + 1) * 1024].rearrange("p (k n) -> p k n", k=2),
                 a["w1"][e].rearrange("(k p) n -> p k n", p=128), s_e)
            t_we = load(S, W2[:, e * 1024:(e + 1) * 1024].rearrange("p (k n) -> p k n", k=4),
                        a["w2"][e].rearrange("(k p) n -> p k n", p=128), s_e)
        t_y = layernorm(Y, X, [tX])
        assert top[0] <= base_top
        meet(t_xd)
        top[0] = base_top
        yT = [mk(2, 128) for _ in range(2)]
        OH = mk(2 * NB, 16)
        s1 = OH[:, 0:NB, :]
        s3 = OH[:, NB:2 * NB, :]
        free = {i: None for i in range(8)}
        lgm = {}
        t_yt = {}

        def turn(b):
            bank = 6 + b % 2
            free[bank] = t_yt[b] = transpose_rows(Y, b, yT[b % 2], bank, t_y[b],
                                                  *(fw(bank) + ([lgm[b - 2]] if b >= 2 else [])))

        turn(0)
        for b in range(NB):
            if b + 1 < NB:
                turn(b + 1)
            bank = b % 2
            T.w(t_yt[b], tw, *fw(bank))
            for k in range(2):
                ins = T.e.matmul(PS[:, bank, 0:16], lhsT=yT[b % 2][:, k, :], rhs=gw[:, k, :], start=(k == 0), stop=(k == 1))
            tt = lgm[b] = T.did(ins)
            free[bank] = t_lg = V.did(V.w(tt).tensor_tensor(lgt[:, b, :], PS[:, bank, 0:16], gbb, ALU.add))
        m1, m2, ew, wa = (mm[:, i, :] for i in range(4))
        t0 = V.did(V.e.memset(rst, 1.0))
        t_rst = V.did(V.w(t0).memset(rst[:, :, 0:1], 0.0))

        def over(v):
            return bc(v.unsqueeze(2), [128, NB, 16])

        def first_max(dst, val, mx, tk):
            tk = V.did(V.w(tk).tensor_tensor(dst, val, over(mx), ALU.is_equal))
            tk = V.did(V.w(tk, t_rst).tensor_tensor_scan(s2.rearrange("p b e -> p (b e)"), rst.rearrange("p b e -> p (b e)"),
                                                         dst.rearrange("p b e -> p (b e)"), 0.0, ALU.mult, ALU.add))
            return V.did(V.w(tk).scalar_tensor_tensor(dst, s2, 1.0, dst, ALU.is_equal, ALU.mult))

        tk = V.did(V.w(t_lg).tensor_reduce(m1, lgt, AX, ALU.max))
        tk = first_max(s1, lgt, m1, tk)
        tk = V.did(V.w(tk).scalar_tensor_tensor(lgt, s1, -3.0e38, lgt, ALU.mult, ALU.add))
        tk = V.did(V.w(tk).tensor_reduce(m2, lgt, AX, ALU.max))
        t_s3 = first_max(s3, lgt, m2, tk)
        tk = V.did(V.w(t_s3).tensor_tensor(ew, m2, m1, ALU.subtract))
        tk = A.did(A.w(tk).activation(ew, ew, ACT.Exp))
        tk = V.did(V.w(tk).tensor_scalar(wa, ew, 1.0, None, ALU.add))
        tk = V.did(V.w(tk).reciprocal(wa, wa))
        tk = V.did(V.w(tk).tensor_tensor(ew, ew, wa, ALU.mult))
        t1 = V.did(V.w(tk).tensor_tensor(lgt, s1, over(wa), ALU.mult))
        t2 = V.did(V.w(tk).tensor_tensor(gt, s3, over(ew), ALU.mult))
        t_gt = V.did(V.w(t1, t2).tensor_tensor(gt, gt, lgt, ALU.add))
        V.did(V.w(t_gt).tensor_scalar(s1[:, 24, :], s1[:, 24, :], tailc, None, ALU.mult))
        tk = V.did(V.e.tensor_scalar(s3[:, 24, :], s3[:, 24, :], tailc, None, ALU.mult))
        T.w(*fw(0, 1, 6, 7))
        route_top = top[0]
        pos, posi, t_pos, eid, t_eid = route(OH, 2 * NB, 16, NT1, tk)
        ew4 = mk(2, NT1)
        eo = mk(2, NT1, dt=I32)
        V.did(V.w(t_eid).tensor_copy(ew4[:, 0, :], eid))
        tk = V.did(V.e.tensor_scalar(ew4[:, 1, :], eid, 4.0, None, ALU.mult))
        t_eo = V.did(V.w(tk).tensor_copy(eo, ew4))
        GRP = 5
        s_sc = [new_sem() for _ in range(NB // GRP)]
        t_sc = {}
        G.w(t_pos, *t_y)
        for b in range(NB):
            n = rows_of(b)
            for c in (b, NB + b):
                t_sc[b // GRP] = s_sc[b // GRP].add(G.e.indirect_dma_start(
                    XSR[:, :], bass.IndirectOffsetOnAxis(ap=posi[0:n, c:c + 1], axis=0), Y[0:n, b, :], None), 16)
        t_gcp = {}
        for b in range(NB):
            r = b % 2
            tt = T.did(T.w(t_gt, *fw(6 + r)).transpose(PS[0:16, 6 + r, 0:128], gt[:, b, :], ident))
            tk = free[6 + r] = A.did(A.w(tt, *([t_gcp[b - 2]] if b >= 2 else [])).activation(
                gT[r][0:16], PS[0:16, 6 + r, 0:128], ACT.Copy))
            tt = t_gcp[b] = T.did(T.w(tk, tw, *fw(4 + r)).matmul(PS[:, 4 + r, 0:256], lhsT=gT[r][0:16], rhs=b2[0:16],
                                                                 start=True, stop=True))
            free[4 + r] = t_bias = V.did(V.w(tt, t_sc[b // GRP]).tensor_tensor(
                Y[:, b, :], Y[:, b, :], PS[:, 4 + r, 0:256], ALU.add))
        T.w(*fw(4, 5, 6, 7))
        V.w(t_pos)
        NX = 3
        after_route, top[0] = top[0], route_top
        xs = [mk(256) for _ in range(NX)]
        xT = [mk(2, 128) for _ in range(2)]
        hr = [mk(512) for _ in range(2)]
        assert top[0] <= route_top + 3 * 800
        top[0] = after_route
        og = [mk(256) for _ in range(2)]
        assert top[0] <= x_top
        s_xs = [new_sem() for _ in range(NX)]
        s_og = [new_sem(), new_sem()]
        pregs = [nc.tensor.alloc_register(f"mx{i}") for i in range(16)]
        aregs = [nc.scalar.alloc_register(f"ma{i}") for i in range(8)]
        t_x, t_xt, t_xe, t_m1, t_h, t_ht, t_hte, t_m2, t_o, t_st = ({} for _ in range(10))

        def xload(i):
            t_x[i] = load(S, xs[i % NX], XSR[i * 128:(i + 1) * 128, :], s_xs[i % NX], *t_sc.values(),
                          *([t_xt[i - NX]] if i >= NX else []))

        def xtrans(i):
            r = i % 2
            T.w(t_x[i], *([t_xe[i - 2]] if i >= 2 else []))
            for f in range(2):
                ins = T.e.transpose(PS[:, r, f * 128:(f + 1) * 128], xs[i % NX][:, f * 128:(f + 1) * 128], ident)
            t_xt[i] = T.did(ins)
            t_xe[i] = V.did(V.w(t_xt[i], *([t_m1[i - 2]] if i >= 2 else [])).tensor_copy(
                xT[r], PS[:, r, 0:256].rearrange("p (f n) -> p f n", f=2)))

        for i in range(NX):
            xload(i)
        xtrans(0)
        for i in range(NT1 + 2):
            if i < NT1:
                r = i % 2
                T.w(t_xe[i], t_we, t_eo, *([t_h[i - 2]] if i >= 2 else []))
                if i % 8 == 0:
                    T.e.reg_load(pregs[i % 16:i % 16 + 8], eo[0:1, 0, i:i + 8])
                v = T.e.snap(pregs[i % 16], min_val=0, max_val=15)
                for k in range(2):
                    ins = T.e.matmul(PS[:, 2 + r, :], lhsT=xT[r][:, k, :], rhs=W1[:, bass.ds(v * 1024 + k * 512, 512)],
                                     start=(k == 0), stop=(k == 1))
                t_m1[i] = T.did(ins)
                t_h[i] = V.did(V.w(t_m1[i], *([t_ht[i - 2]] if i >= 2 else [])).tensor_copy(hr[r], PS[:, 2 + r, :]))
            if i >= 1 and i - 1 < NT1:
                j = i - 1
                r = j % 2
                T.w(t_h[j], *([t_hte[j - 2]] if j >= 2 else []))
                for k in range(4):
                    ins = T.e.transpose(PS[:, 4 + r, k * 128:(k + 1) * 128], hr[r][:, k * 128:(k + 1) * 128], ident)
                t_ht[j] = T.did(ins)
                A.w(t_ht[j], t_eo, *([t_m2[j - 3]] if j >= 3 else []))
                if j % 8 == 0:
                    A.e.reg_load(aregs, eo[0:1, 1, j:j + 8])
                v = A.e.snap(aregs[j % 8], min_val=0, max_val=60)
                for k in range(4):
                    t_hte[j] = A.did(A.e.activation(hT[j % 3][:, k, :], PS[:, 4 + r, k * 128:(k + 1) * 128], ACT.Relu,
                                                    bias=b1c[:, bass.ds(v + k, 1)]))
            if i + 1 < NT1:
                xtrans(i + 1)
                if i + 1 + NX - 1 < NT1 and i + NX not in t_x:
                    xload(i + NX)
            if i >= 2:
                j = i - 2
                r = j % 2
                T.w(t_hte[j], *([t_o[j - 2]] if j >= 2 else []))
                v = T.e.snap(pregs[j % 16], min_val=0, max_val=15)
                for k in range(4):
                    ins = T.e.matmul(PS[:, 6 + r, 0:256], lhsT=hT[j % 3][:, k, :], rhs=W2[:, bass.ds(v * 1024 + k * 256, 256)],
                                     start=(k == 0), stop=(k == 3))
                t_m2[j] = T.did(ins)
                t_o[j] = V.did(V.w(t_m2[j], *([t_st[j - 2]] if j >= 2 else [])).tensor_copy(og[r], PS[:, 6 + r, 0:256]))
                t_st[j] = load(S, YSR[j * 128:(j + 1) * 128, :], og[r], s_og[r], t_o[j])
        meet(t_st[NT1 - 1], t_st[NT1 - 2])
        NRG = 8
        yg = [W1[:, i * 256:(i + 1) * 256] for i in range(NRG)]
        X = W2[:, 0:NB * D].rearrange("p (b d) -> p b d", b=NB)
        t_xl = load(S, W2[:, 0:NB * D], XD[:, :], s_xd)
        s_yg = [new_sem() for _ in range(NRG)]
        t_use = {}
        at = NRG * 256
        st = W1[:, at:at + NB * 6].rearrange("p (b n) -> p b n", b=NB)
        mv = W1[:, at + 200:at + 200 + NB * 2].rearrange("p (b n) -> p b n", b=NB)
        sd = W1[:, at + 300:at + 300 + NB]
        gm, bt = W1[:, at + 512:at + 768], W1[:, at + 768:at + 1024]
        load(S, gm, a["gamma"].unsqueeze(0).partition_broadcast(128), s_xd)
        tw = load(S, bt, a["beta"].unsqueeze(0).partition_broadcast(128), s_xd)
        s_o = new_sem()
        for b in range(NB):
            n = rows_of(b)
            for k, g in ((0, wa), (1, ew)):
                u = 2 * b + k
                buf = yg[u % NRG]
                G.w(*([t_use[u - NRG]] if u >= NRG else []))
                tg_ = s_yg[u % NRG].add(G.e.indirect_dma_start(
                    buf[0:n], None, YSR[:, :], bass.IndirectOffsetOnAxis(ap=posi[0:n, k * NB + b:k * NB + b + 1], axis=0)), 16)
                tk = t_use[u] = V.did(V.w(tg_, *([tk] if k else [])).scalar_tensor_tensor(
                    Y[0:n, b, :], buf[0:n], g[0:n, b:b + 1], Y[0:n, b, :], ALU.mult, ALU.add))
            tk = V.did(V.w(tk).bn_stats(st[:, b, :], Y[:, b, :]))
            tk = V.did(V.w(tk).bn_aggr(mv[:, b, :], st[:, b, :]))
            if b % GRP == GRP - 1:
                b0 = b - GRP + 1
                tk = A.did(A.w(tk).activation(sd[:, b0:b + 1], mv[:, b0:b + 1, 1], ACT.Sqrt, bias=epsc))
                V.w(t_xl, tw)
                for c in range(b0, b + 1):
                    V.did(V.e.tensor_tensor(X[:, c, :], X[:, c, :], bt, ALU.add))
                tk = V.did(V.w(tk).reciprocal(sd[:, b0:b + 1], sd[:, b0:b + 1]))
                t_n = [V.did(V.w(tk).scalar_tensor_tensor(Y[:, c, :], Y[:, c, :], mv[:, c, 0:1], gm,
                                                          ALU.subtract, ALU.mult)) for c in range(b0, b + 1)]
                for i, c in enumerate(range(b0, b + 1)):
                    tk = V.did(V.w(t_n[i]).scalar_tensor_tensor(Y[:, c, :], Y[:, c, :], sd[:, c:c + 1], X[:, c, :],
                                                                ALU.mult, ALU.add))
                hi = min(b + 1, NB - 1)
                to = load(S, out[b0 * 128:hi * 128, :].rearrange("(b p) d -> p b d", p=128), Y[:, b0:hi, :], s_o, tk)
        to = load(S, out[3072:N, :], Y[0:TAIL, 24, :], s_o)
        S.w(to)


def constants():
    e = np.arange(128)
    sq = np.zeros((128, 5, 128), np.float32)
    sq[:, 0] = np.eye(128)
    sq[:, 1] = e[None, :]
    sq[:, 2] = e[None, :] < e[:, None]
    sq[:, 3] = e[:, None] < e[None, :]
    sq[:, 4] = 1.0
    mask = np.zeros((128, 2, 8), np.float32)
    for f in range(2):
        for p in range(128):
            mask[p, f, (f * 128 + p) // 32] = 1.0
    return {
        "c_sq": sq,
        "c_pairs": np.tile(np.arange(T2 // 2, dtype=np.float32)[None, :], (128, 1)),
        "c_pidx": e.astype(np.float32)[:, None],
        "c_eps": np.full((128, 1), 1e-5, np.float32),
        "c_mask": mask,
        "c_tail": (e < TAIL).astype(np.float32)[:, None],
        "c_tok": (np.arange(NB)[None, :] * 128 + e[:, None]).astype(np.int32),
    }


def tiles(v, pad):
    return np.pad(v, (0, 128 * T1 - len(v)), constant_values=pad).reshape(T1, 128).T


def arrays_of(i):
    c = np.ascontiguousarray
    g = {k: np.asarray(v) for k, v in i.items()}
    w = g["L1_gnn_a"].reshape(8, 5, 32)
    r = {
        "x": g["x"], "src": g["src"], "dst": g["dst"], "edge_weight": g["edge_weight"],
        "srcP": tiles(g["src"], PADKEY), "dstP": tiles(g["dst"], PADKEY),
        "nextP": tiles(g["dst"][1:], PADKEY), "wP": tiles(g["edge_weight"], 0),
        "weightT": g["L0_gnn_weight"].transpose(0, 2, 1), "w_ihT": g["L0_gnn_w_ih"].T, "w_hhT": g["L0_gnn_w_hh"].T,
        "b_ih": g["L0_gnn_b_ih"], "b_hh": g["L0_gnn_b_hh"],
        "W1": g["L0_ffn_W1"], "b1T": g["L0_ffn_b1"].reshape(8, 128).T, "Wg": g["L0_ffn_Wg"], "bg": g["L0_ffn_bg"],
        "Wd": g["L0_ffn_Wd"], "bd": g["L0_ffn_bd"],
        "Wgat": g["L1_gnn_W"].transpose(1, 0, 2).reshape(256, 256),
        "a5": w.transpose(1, 0, 2).reshape(5, 256),
        "a4c": w[:, 3].reshape(2, 128).T, "a5c": w[:, 4].reshape(2, 128).T,
        "gate_w": g["L1_ffn_gate_w"], "gate_b": g["L1_ffn_gate_b"], "w1": g["L1_ffn_w1"],
        "b1m": g["L1_ffn_b1"].reshape(16, 4, 128).transpose(2, 0, 1), "w2": g["L1_ffn_w2"], "b2": g["L1_ffn_b2"],
        "gamma": g["L1_ffn_gamma"], "beta": g["L1_ffn_beta"],
    }
    return {k: c(v) for k, v in r.items()} | constants()


def kernel(**inputs):
    import concourse.bacc as bacc
    from concourse.bass_utils import run_bass_kernel_spmd

    nc = bacc.Bacc("TRN2", target_bir_lowering=False, num_devices=1)
    arrays = arrays_of(inputs)
    aps = {k: nc.dram_tensor(k, v.shape, mybir.dt.from_np(v.dtype), kind="ExternalInput").ap() for k, v in arrays.items()}
    out = nc.dram_tensor("out", (N, D), F32, kind="ExternalOutput").ap()
    program(nc, aps, out)
    r = run_bass_kernel_spmd(nc, [arrays], core_ids=[0])
    return r.results[0]["out"]
```
